# Optimizing a Trainium2 kernel written in Bass

```python
import numpy as np
import jax
import jax.numpy as jnp

def _softmax(x, axis=-1):
    return jax.nn.softmax(x, axis=axis)

def _gelu(x):
    return jax.nn.gelu(x, approximate=True)

def _silu(x):
    return jax.nn.silu(x)

def _sigmoid(x):
    return jax.nn.sigmoid(x)

def _layernorm(x, axis=-1, eps=1e-05):
    m = jnp.mean(x, axis=axis, keepdims=True)
    v = jnp.var(x, axis=axis, keepdims=True)
    return (x - m) / jnp.sqrt(v + eps)

def _scatter_add(tgt, idx, src, axis=0):
    return tgt.at[idx].add(src)

def _segment_sum(src, seg, n):
    return jax.ops.segment_sum(src, seg, n)
kernel_name = 'mk_dlrm_tower_d1_rec_r8_c48d35'

def setup_inputs(seed: int=0):
    np.random.seed(seed)
    _w = jnp.asarray

    def _rec_inputs():
        import jax
        import jax.numpy as jnp
        _tk = jax.random.key(seed)
        dense_ctx = jax.random.normal(jax.random.fold_in(_tk, 190), (1024, 16), jnp.float32)
        ids = jnp.stack([jax.random.randint(jax.random.fold_in(_tk, 200 + f), (1024,), 0, v, jnp.int32) for f, v in enumerate([125000, 1250, 1000, 1250, 125000, 12500, 1250, 125000, 1000, 1250, 12500, 1000, 125000, 125000, 1250, 12500, 1000, 125000, 1250, 1000, 12500, 125000, 1250, 1000, 125000, 12500, 1250, 1250, 12500, 12500, 12500, 1250, 1000, 125000, 125000, 125000, 1250, 12500, 125000])], axis=1)
        tbl_0 = 0.05 * jax.random.normal(jax.random.fold_in(_tk, 500 + 0), (125000, 16), jnp.float32)
        tbl_1 = 0.05 * jax.random.normal(jax.random.fold_in(_tk, 500 + 1), (1250, 16), jnp.float32)
        tbl_2 = 0.05 * jax.random.normal(jax.random.fold_in(_tk, 500 + 2), (1000, 16), jnp.float32)
        tbl_3 = 0.05 * jax.random.normal(jax.random.fold_in(_tk, 500 + 3), (1250, 16), jnp.float32)
        tbl_4 = 0.05 * jax.random.normal(jax.random.fold_in(_tk, 500 + 4), (125000, 16), jnp.float32)
        tbl_5 = 0.05 * jax.random.normal(jax.random.fold_in(_tk, 500 + 5), (12500, 16), jnp.float32)
        tbl_6 = 0.05 * jax.random.normal(jax.random.fold_in(_tk, 500 + 6), (1250, 16), jnp.float32)
        tbl_7 = 0.05 * jax.random.normal(jax.random.fold_in(_tk, 500 + 7), (125000, 16), jnp.float32)
        tbl_8 = 0.05 * jax.random.normal(jax.random.fold_in(_tk, 500 + 8), (1000, 16), jnp.float32)
        tbl_9 = 0.05 * jax.random.normal(jax.random.fold_in(_tk, 500 + 9), (1250, 16), jnp.float32)
        tbl_10 = 0.05 * jax.random.normal(jax.random.fold_in(_tk, 500 + 10), (12500, 16), jnp.float32)
        tbl_11 = 0.05 * jax.random.normal(jax.random.fold_in(_tk, 500 + 11), (1000, 16), jnp.float32)
        tbl_12 = 0.05 * jax.random.normal(jax.random.fold_in(_tk, 500 + 12), (125000, 16), jnp.float32)
        tbl_13 = 0.05 * jax.random.normal(jax.random.fold_in(_tk, 500 + 13), (125000, 16), jnp.float32)
        tbl_14 = 0.05 * jax.random.normal(jax.random.fold_in(_tk, 500 + 14), (1250, 16), jnp.float32)
        tbl_15 = 0.05 * jax.random.normal(jax.random.fold_in(_tk, 500 + 15), (12500, 16), jnp.float32)
        tbl_16 = 0.05 * jax.random.normal(jax.random.fold_in(_tk, 500 + 16), (1000, 16), jnp.float32)
        tbl_17 = 0.05 * jax.random.normal(jax.random.fold_in(_tk, 500 + 17), (125000, 16), jnp.float32)
        tbl_18 = 0.05 * jax.random.normal(jax.random.fold_in(_tk, 500 + 18), (1250, 16), jnp.float32)
        tbl_19 = 0.05 * jax.random.normal(jax.random.fold_in(_tk, 500 + 19), (1000, 16), jnp.float32)
        tbl_20 = 0.05 * jax.random.normal(jax.random.fold_in(_tk, 500 + 20), (12500, 16), jnp.float32)
        tbl_21 = 0.05 * jax.random.normal(jax.random.fold_in(_tk, 500 + 21), (125000, 16), jnp.float32)
        tbl_22 = 0.05 * jax.random.normal(jax.random.fold_in(_tk, 500 + 22), (1250, 16), jnp.float32)
        tbl_23 = 0.05 * jax.random.normal(jax.random.fold_in(_tk, 500 + 23), (1000, 16), jnp.float32)
        tbl_24 = 0.05 * jax.random.normal(jax.random.fold_in(_tk, 500 + 24), (125000, 16), jnp.float32)
        tbl_25 = 0.05 * jax.random.normal(jax.random.fold_in(_tk, 500 + 25), (12500, 16), jnp.float32)
        tbl_26 = 0.05 * jax.random.normal(jax.random.fold_in(_tk, 500 + 26), (1250, 16), jnp.float32)
        tbl_27 = 0.05 * jax.random.normal(jax.random.fold_in(_tk, 500 + 27), (1250, 16), jnp.float32)
        tbl_28 = 0.05 * jax.random.normal(jax.random.fold_in(_tk, 500 + 28), (12500, 16), jnp.float32)
        tbl_29 = 0.05 * jax.random.normal(jax.random.fold_in(_tk, 500 + 29), (12500, 16), jnp.float32)
        tbl_30 = 0.05 * jax.random.normal(jax.random.fold_in(_tk, 500 + 30), (12500, 16), jnp.float32)
        tbl_31 = 0.05 * jax.random.normal(jax.random.fold_in(_tk, 500 + 31), (1250, 16), jnp.float32)
        tbl_32 = 0.05 * jax.random.normal(jax.random.fold_in(_tk, 500 + 32), (1000, 16), jnp.float32)
        tbl_33 = 0.05 * jax.random.normal(jax.random.fold_in(_tk, 500 + 33), (125000, 16), jnp.float32)
        tbl_34 = 0.05 * jax.random.normal(jax.random.fold_in(_tk, 500 + 34), (125000, 16), jnp.float32)
        tbl_35 = 0.05 * jax.random.normal(jax.random.fold_in(_tk, 500 + 35), (125000, 16), jnp.float32)
        tbl_36 = 0.05 * jax.random.normal(jax.random.fold_in(_tk, 500 + 36), (1250, 16), jnp.float32)
        tbl_37 = 0.05 * jax.random.normal(jax.random.fold_in(_tk, 500 + 37), (12500, 16), jnp.float32)
        tbl_38 = 0.05 * jax.random.normal(jax.random.fold_in(_tk, 500 + 38), (125000, 16), jnp.float32)
        _rk = jax.random.fold_in(_tk, 7)
        W_top1 = 0.05 * jax.random.normal(jax.random.fold_in(_tk, 801), (400, 512), jnp.float32)
        W_top2 = 0.0441942 * jax.random.normal(jax.random.fold_in(_tk, 802), (512, 256), jnp.float32)
        W_top3 = 0.0625 * jax.random.normal(jax.random.fold_in(_tk, 803), (256, 1), jnp.float32)
        b_top1 = jnp.zeros((512,), jnp.float32)
        b_top2 = jnp.zeros((256,), jnp.float32)
        return (dense_ctx, ids, tbl_0, tbl_1, tbl_2, tbl_3, tbl_4, tbl_5, tbl_6, tbl_7, tbl_8, tbl_9, tbl_10, tbl_11, tbl_12, tbl_13, tbl_14, tbl_15, tbl_16, tbl_17, tbl_18, tbl_19, tbl_20, tbl_21, tbl_22, tbl_23, tbl_24, tbl_25, tbl_26, tbl_27, tbl_28, tbl_29, tbl_30, tbl_31, tbl_32, tbl_33, tbl_34, tbl_35, tbl_36, tbl_37, tbl_38, W_top1, b_top1, W_top2, b_top2, W_top3)
    dense_ctx, ids, tbl_0, tbl_1, tbl_2, tbl_3, tbl_4, tbl_5, tbl_6, tbl_7, tbl_8, tbl_9, tbl_10, tbl_11, tbl_12, tbl_13, tbl_14, tbl_15, tbl_16, tbl_17, tbl_18, tbl_19, tbl_20, tbl_21, tbl_22, tbl_23, tbl_24, tbl_25, tbl_26, tbl_27, tbl_28, tbl_29, tbl_30, tbl_31, tbl_32, tbl_33, tbl_34, tbl_35, tbl_36, tbl_37, tbl_38, W_top1, b_top1, W_top2, b_top2, W_top3 = _rec_inputs()

    def _L0_rec_setup():
        import jax, jax.numpy as jnp
        import numpy as np
        B, F0, D = (512, 39, 16)
        CIN = [128, 128, 128]

        def _cin_layer(X0, Xi, W, b):
            H = W.shape[0]
            F0_, Fi = (X0.shape[1], Xi.shape[1])
            Wr = W.reshape(H, F0_, Fi)
            return jnp.einsum('hjk,bjd,bkd->bhd', Wr, X0, Xi) + b[None, :, None]
        key = jax.random.key(seed)
        ks = jax.random.split(key, 4)
        x = jax.random.normal(ks[0], (B, F0, D), dtype=jnp.float32)
        fields = [F0] + CIN
        inp = {'embedded_features': x}
        for i in range(len(CIN)):
            cin = F0 * fields[i]
            cout = fields[i + 1]
            kw = jax.random.fold_in(ks[1], i)
            inp[f'W{i}'] = jax.random.normal(kw, (cout, cin), dtype=jnp.float32) / np.sqrt(cin)
            inp[f'b{i}'] = jnp.zeros((cout,), dtype=jnp.float32)
        return inp
    _L0_rec_all = _L0_rec_setup()
    _L0_rec_in = {k: v for k, v in _L0_rec_all.items() if k in ('W0', 'b0', 'W1', 'b1', 'W2', 'b2')}
    del _L0_rec_all
    return {'dense_ctx': dense_ctx, 'ids': ids, 'tbl_0': tbl_0, 'tbl_1': tbl_1, 'tbl_2': tbl_2, 'tbl_3': tbl_3, 'tbl_4': tbl_4, 'tbl_5': tbl_5, 'tbl_6': tbl_6, 'tbl_7': tbl_7, 'tbl_8': tbl_8, 'tbl_9': tbl_9, 'tbl_10': tbl_10, 'tbl_11': tbl_11, 'tbl_12': tbl_12, 'tbl_13': tbl_13, 'tbl_14': tbl_14, 'tbl_15': tbl_15, 'tbl_16': tbl_16, 'tbl_17': tbl_17, 'tbl_18': tbl_18, 'tbl_19': tbl_19, 'tbl_20': tbl_20, 'tbl_21': tbl_21, 'tbl_22': tbl_22, 'tbl_23': tbl_23, 'tbl_24': tbl_24, 'tbl_25': tbl_25, 'tbl_26': tbl_26, 'tbl_27': tbl_27, 'tbl_28': tbl_28, 'tbl_29': tbl_29, 'tbl_30': tbl_30, 'tbl_31': tbl_31, 'tbl_32': tbl_32, 'tbl_33': tbl_33, 'tbl_34': tbl_34, 'tbl_35': tbl_35, 'tbl_36': tbl_36, 'tbl_37': tbl_37, 'tbl_38': tbl_38, 'W_top1': W_top1, 'b_top1': b_top1, 'W_top2': W_top2, 'b_top2': b_top2, 'W_top3': W_top3, 'L0_rec_W0': _L0_rec_in['W0'], 'L0_rec_b0': _L0_rec_in['b0'], 'L0_rec_W1': _L0_rec_in['W1'], 'L0_rec_b1': _L0_rec_in['b1'], 'L0_rec_W2': _L0_rec_in['W2'], 'L0_rec_b2': _L0_rec_in['b2']}

def reference(dense_ctx, ids, tbl_0, tbl_1, tbl_2, tbl_3, tbl_4, tbl_5, tbl_6, tbl_7, tbl_8, tbl_9, tbl_10, tbl_11, tbl_12, tbl_13, tbl_14, tbl_15, tbl_16, tbl_17, tbl_18, tbl_19, tbl_20, tbl_21, tbl_22, tbl_23, tbl_24, tbl_25, tbl_26, tbl_27, tbl_28, tbl_29, tbl_30, tbl_31, tbl_32, tbl_33, tbl_34, tbl_35, tbl_36, tbl_37, tbl_38, W_top1, b_top1, W_top2, b_top2, W_top3, L0_rec_W0, L0_rec_b0, L0_rec_W1, L0_rec_b1, L0_rec_W2, L0_rec_b2):
    import jax
    import jax.numpy as jnp

    def _L0_rec_ref(embedded_features, W0, b0, W1, b1, W2, b2):
        import jax, jax.numpy as jnp
        import numpy as np
        B, F0, D = (512, 39, 16)
        CIN = [128, 128, 128]

        def _cin_layer(X0, Xi, W, b):
            H = W.shape[0]
            F0_, Fi = (X0.shape[1], Xi.shape[1])
            Wr = W.reshape(H, F0_, Fi)
            return jnp.einsum('hjk,bjd,bkd->bhd', Wr, X0, Xi) + b[None, :, None]
        X0 = embedded_features
        Ws = [(W0, b0), (W1, b1), (W2, b2)]
        Xi = X0
        res = []
        for W, b in Ws:
            Xi = _cin_layer(X0, Xi, W, b)
            res.append(Xi.sum(axis=2))
        return jnp.concatenate(res, axis=1)
    e = jnp.stack([tbl_0[ids[:, 0]], tbl_1[ids[:, 1]], tbl_2[ids[:, 2]], tbl_3[ids[:, 3]], tbl_4[ids[:, 4]], tbl_5[ids[:, 5]], tbl_6[ids[:, 6]], tbl_7[ids[:, 7]], tbl_8[ids[:, 8]], tbl_9[ids[:, 9]], tbl_10[ids[:, 10]], tbl_11[ids[:, 11]], tbl_12[ids[:, 12]], tbl_13[ids[:, 13]], tbl_14[ids[:, 14]], tbl_15[ids[:, 15]], tbl_16[ids[:, 16]], tbl_17[ids[:, 17]], tbl_18[ids[:, 18]], tbl_19[ids[:, 19]], tbl_20[ids[:, 20]], tbl_21[ids[:, 21]], tbl_22[ids[:, 22]], tbl_23[ids[:, 23]], tbl_24[ids[:, 24]], tbl_25[ids[:, 25]], tbl_26[ids[:, 26]], tbl_27[ids[:, 27]], tbl_28[ids[:, 28]], tbl_29[ids[:, 29]], tbl_30[ids[:, 30]], tbl_31[ids[:, 31]], tbl_32[ids[:, 32]], tbl_33[ids[:, 33]], tbl_34[ids[:, 34]], tbl_35[ids[:, 35]], tbl_36[ids[:, 36]], tbl_37[ids[:, 37]], tbl_38[ids[:, 38]]], axis=1)
    z = _L0_rec_ref(e, L0_rec_W0, L0_rec_b0, L0_rec_W1, L0_rec_b1, L0_rec_W2, L0_rec_b2)
    z = z.reshape(z.shape[0], -1)
    h = jnp.concatenate([z, dense_ctx], axis=1)
    h = jnp.maximum(h @ W_top1 + b_top1, 0.0)
    h = jnp.maximum(h @ W_top2 + b_top2, 0.0)
    y = h @ W_top3
    return y

_drawn_inputs = setup_inputs


def setup_inputs(seed=0):
    import zlib

    import numpy as np

    out = dict(_drawn_inputs(seed))
    spreads = {'b_top1': (0.0, 0.1),
     'b_top2': (0.0, 0.1),
     'L0_rec_b0': (0.0, 0.1),
     'L0_rec_b1': (0.0, 0.1),
     'L0_rec_b2': (0.0, 0.1)}
    factors = {'tbl_0': 8.0,
     'tbl_1': 5.805,
     'tbl_2': 4.934,
     'tbl_3': 7.056,
     'tbl_4': 8.0,
     'tbl_5': 8.0,
     'tbl_6': 8.0,
     'tbl_7': 6.799,
     'tbl_8': 8.0,
     'tbl_9': 8.0,
     'tbl_10': 8.0,
     'tbl_11': 6.719,
     'tbl_12': 8.0,
     'tbl_13': 8.0,
     'tbl_14': 4.221,
     'tbl_15': 5.35,
     'tbl_16': 8.0,
     'tbl_17': 8.0,
     'tbl_18': 8.0,
     'tbl_19': 5.767,
     'tbl_20': 7.303,
     'tbl_21': 8.0,
     'tbl_22': 8.0,
     'tbl_23': 8.0,
     'tbl_24': 8.0,
     'tbl_25': 7.191,
     'tbl_26': 5.788,
     'tbl_27': 8.0,
     'tbl_28': 8.0,
     'tbl_29': 8.0,
     'tbl_30': 6.374,
     'tbl_31': 6.127,
     'tbl_32': 8.0,
     'tbl_33': 6.992,
     'tbl_34': 8.0,
     'tbl_35': 7.558,
     'tbl_36': 8.0,
     'tbl_37': 6.434,
     'tbl_38': 8.0,
     'L0_rec_W0': 3.122}
    for name, (base, spread) in spreads.items():
        noise = np.random.default_rng([zlib.crc32(name.encode()), seed]).standard_normal(out[name].shape)
        drawn = base * np.exp(spread * noise) if base else spread * noise
        out[name] = jnp.asarray(drawn.astype(out[name].dtype))
    for name, factor in factors.items():
        out[name] = (out[name] * factor).astype(out[name].dtype)
    return out
```

```python
from contextlib import ExitStack

import concourse.bass as bass
from concourse import mybir

F32 = mybir.dt.float32
F32R = mybir.dt.float32r
I32 = mybir.dt.int32
ALU = mybir.AluOpType
ACT = mybir.ActivationFunctionType
AX = mybir.AxisListType

P = 128
B, F, D, H = 1024, 39, 16, 128
N_CIN = 3
DENSE = 16
TOP1, TOP2 = 512, 256
BLOCK_ROWS = 128
BLOCKS = B // BLOCK_ROWS
BLOCK_COLS = BLOCK_ROWS * D
CHUNKS = 4
CHUNK = BLOCK_COLS // CHUNKS
TILES = BLOCK_COLS // P
TPC = TILES // CHUNKS
TILE_ROWS = P // D
COPIES = 3
PAIRS = COPIES * F
UNITS = -(-(F // 2 + 1) // COPIES)
LO = 64
SPLIT = LO + F
JB = 4
BANKS = -(-F // JB)
T_RING = 4
J1 = F + 1
JPAD = 40

ACT_BANKS = (1, 4, 7)
FIELDS_OF = [min(JB, F - JB * q) for q in range(BANKS)]
DVE_BANKS = tuple(q for q in range(BANKS) if q not in ACT_BANKS)
DVE_UNITS = sum(FIELDS_OF[q] for q in DVE_BANKS)
DVE_STEPS = DVE_UNITS + 2
GP_STEPS = 4
ETR = 4
L2_FROM, L2_SLOTS, L2_EACH = 11, 14, 3
SLOTS = TILES * BANKS
CHUNK_SLOTS = TPC * BANKS


def dve_units_before(q):
    return sum(FIELDS_OF[x] for x in DVE_BANKS if x < q)


def act_banks_before(q):
    return sum(1 for x in ACT_BANKS if x < q)


def cin_tower(nc, ids, dense_t, w0_fwd, w0_rev, w1, w2, b0, b1_rows, b2, select, ident, mask,
              w_top1, w_top1_dense, b_top1, w_top2, b_top2, w_top3, out, tables):
    with ExitStack() as ctx:
        def sb(name, shape, dt=F32):
            return ctx.enter_context(nc.sbuf_tensor(name, shape, dt))

        def bank(name):
            return ctx.enter_context(nc.psum_tensor(name, [P, 512], F32))

        def sem(name):
            return ctx.enter_context(nc.semaphore(name))

        w1_hi = sb("w1_hi", [P, F * H], F32R)
        w1_lo = sb("w1_lo", [P, F * H], F32R)
        w2_sb = sb("w2_sb", [P, F, H])
        w0_hi = sb("w0_hi", [PAIRS, UNITS, H], F32R)
        w0_lo = sb("w0_lo", [PAIRS, UNITS, H], F32R)
        sel = sb("sel", [SPLIT, UNITS + 1, PAIRS], F32R)
        ident_sb = sb("ident_sb", [P, P])
        mask_sb = sb("mask_sb", [P, TILE_ROWS, JPAD])
        b0_sb = sb("b0_sb", [P, 1])
        b1_sb = sb("b1_sb", [P, H])
        b2_sb = sb("b2_sb", [P, 1])
        b0_d = sb("b0_d", [P, 1])
        b2_d = sb("b2_d", [P, 1])
        wt1 = sb("wt1", [P, N_CIN, TOP1])
        wt1_dense = sb("wt1_dense", [DENSE, TOP1])
        wt2 = sb("wt2", [P, TOP1 // P, TOP2])
        wt3 = sb("wt3", [P, TOP2 // P])
        bt1 = sb("bt1", [P, TOP1 // P])
        bt2 = sb("bt2", [P, TOP2 // P])
        ids_cur = sb("ids_cur", [P, F], I32)
        emb = sb("emb", [P, F * D])
        x0 = sb("x0", [SPLIT, BLOCK_COLS], F32R)
        x0_copies = sb("x0_copies", [PAIRS, CHUNK])
        x0_t = sb("x0_t", [P, TILES, JPAD])
        z = sb("z", [PAIRS, 2, CHUNK])
        z_hi = sb("z_hi", [PAIRS, 2, CHUNK], F32R)
        z_lo = sb("z_lo", [PAIRS, 2, CHUNK], F32R)
        x1_hi = sb("x1_hi", [P, BLOCK_COLS], F32R)
        x1_lo = sb("x1_lo", [P, BLOCK_COLS], F32R)
        prod = sb("prod", [P, 2, len(ACT_BANKS), JB * H])
        gp_sum = sb("gp_sum", [P, 2, H])
        dve_sum = sb("dve_sum", [P, 2, 2, H])
        x2 = sb("x2", [P, 4, H])
        x0_diag = sb("x0_diag", [P, 4, TILE_ROWS, JPAD])
        y_sb = sb("y_sb", [P, JPAD, BLOCK_ROWS])
        feat = sb("feat", [P, N_CIN, B])
        dense = sb("dense", [DENSE, B])
        h1 = sb("h1", [P, TOP1 // P, 512])
        h2 = sb("h2", [P, TOP2 // P, 512])
        y_out = sb("y_out", [1, B])
        w1_raw = y_sb[:, 0:F, :].rearrange("p j h -> p (j h)")
        raw = prod[:, :, :, :].rearrange("p a b c -> p (a b c)")
        n_w0 = UNITS * H
        w0_fwd_raw = raw[0:PAIRS, 0:n_w0]
        w0_rev_raw = raw[0:PAIRS, n_w0:2 * n_w0]
        sel_raw = raw[0:SPLIT, 2 * n_w0:2 * n_w0 + (UNITS + 1) * PAIRS]

        ps_t = [bank(f"ps_t{i}") for i in range(T_RING)]
        ps_sel = bank("ps_sel")
        ps_x1 = bank("ps_x1")
        ps_y = bank("ps_y")
        ps_l2 = bank("ps_l2")

        consts_in = sem("consts_in")
        w0_in = sem("w0_in")
        w1_in = sem("w1_in")
        w2_in = sem("w2_in")
        top_in = sem("top_in")
        ids_in = sem("ids_in")
        emb_in = sem("emb_in")
        out_done = sem("out_done")
        zeroed = sem("zeroed")
        ones_set = sem("ones_set")
        w0_folded = sem("w0_folded")
        w0_split = sem("w0_split")
        sel_cast = sem("sel_cast")
        w1_hi_set = sem("w1_hi_set")
        w1_split = sem("w1_split")
        bias_scaled = sem("bias_scaled")
        emb_turned = sem("emb_turned")
        x0_hi_set = sem("x0_hi_set")
        x0_lo_set = sem("x0_lo_set")
        copies_selected = sem("copies_selected")
        copies_set = sem("copies_set")
        x0_turned = sem("x0_turned")
        x0_t_set = sem("x0_t_set")
        shift_selected = sem("shift_selected")
        z_set = sem("z_set")
        z_hi_set = sem("z_hi_set")
        z_lo_set = sem("z_lo_set")
        z_used = sem("z_used")
        x1_hi_set = sem("x1_hi_set")
        x1_done = sem("x1_done")
        bank_done = sem("bank_done")
        dve_steps = sem("dve_steps")
        act_scaled = sem("act_scaled")
        gp_steps = sem("gp_steps")
        diag_set = sem("diag_set")
        y_done = sem("y_done")
        y_set = sem("y_set")
        l2_done = sem("l2_done")
        l1_feat_set = sem("l1_feat_set")
        l2_feat_set = sem("l2_feat_set")
        feat0_done = sem("feat0_done")
        top_mm = sem("top_mm")
        top_act = sem("top_act")

        block = ctx.enter_context(nc.Block())

        def position(s, q):
            return s * BANKS + q

        def layer0_at(p):
            c = p // CHUNK_SLOTS
            return (0, CHUNKS - 1, p) if c == 0 else (1, c - 1, p % CHUNK_SLOTS)

        @block.sync
        def _(sp):
            sp.dma_start(ids_cur[:, :], ids[0]).then_inc(ids_in, 16)
            sp.dma_start(ident_sb[:, :], ident).then_inc(consts_in, 16)
            sp.dma_start(mask_sb[:, :, :], mask).then_inc(consts_in, 16)
            sp.dma_start(b0_sb[:, :], b0).then_inc(consts_in, 16)
            sp.dma_start(b1_sb[:, :], b1_rows).then_inc(consts_in, 16)
            sp.dma_start(b2_sb[:, :], b2).then_inc(consts_in, 16)
            sp.dma_start(sel_raw, select).then_inc(w0_in, 16)
            sp.dma_start(w0_fwd_raw, w0_fwd).then_inc(w0_in, 16)
            sp.dma_start(w0_rev_raw, w0_rev).then_inc(w0_in, 16)
            sp.dma_start(w1_raw, w1).then_inc(w1_in, 16)
            sp.dma_start(w2_sb[:, :, :], w2).then_inc(w2_in, 16)
            for t, d in ((wt1[:, :, :], w_top1), (wt1_dense[:, :], w_top1_dense), (bt1[:, :], b_top1),
                         (wt2[:, :, :], w_top2), (bt2[:, :], b_top2), (wt3[:, :], w_top3),
                         (dense[:, :], dense_t)):
                sp.dma_start(t, d).then_inc(top_in, 16)
            sp.wait_ge(emb_in, 16 * F)
            sp.dma_start(ids_cur[:, :], ids[1]).then_inc(ids_in, 16)
            with sp.Fori(2, BLOCKS) as k:
                sp.wait_ge(emb_in, 16 * F * k)
                sp.dma_start(ids_cur[:, :], ids[bass.ds(k, 1)].rearrange("a p f -> (a p) f")).then_inc(ids_in, 16)
            sp.wait_ge(top_act, 2 * 7)
            sp.dma_start(out.rearrange("b a -> a b"), y_out[:, :]).then_inc(out_done, 16)
            sp.wait_ge(out_done, 16)

        @block.gpsimd
        def _(gp):
            def gather(f):
                gp.indirect_dma_start(emb[:, D * f:D * f + D], None, tables[f],
                                      bass.IndirectOffsetOnAxis(ap=ids_cur[:, f:f + 1], axis=0)).then_inc(emb_in, 16)

            def layer0(k, c, u):
                t, r = divmod(u - 7, 4)
                if r == 0 and 0 <= t < UNITS:
                    n = (k * CHUNKS + c) * UNITS + t
                    b = (c * UNITS + t) % 2
                    gp.wait_ge(z_hi_set, n + 1)
                    if not (isinstance(n, int) and n < 2):
                        gp.wait_ge(z_used, n - 1)
                    gp.tensor_tensor(z_lo[:, b, :], z[:, b, :], z_hi[:, b, :].bitcast(F32),
                                     ALU.subtract).then_inc(z_lo_set, 1)

            def block_of(k, first, prepares, gathers):
                for p in range(SLOTS):
                    s, q = divmod(p, BANKS)
                    g = TILES * k + s
                    pair = prod[:, s % 2]
                    if q == 2:
                        if s % TPC == 0:
                            gp.wait_ge(x0_t_set, CHUNKS * k + s // TPC + 1)
                        if s >= 4 or not first:
                            gp.wait_ge(y_done, g - 3)
                        gp.tensor_tensor(x0_diag[:, s % 4], x0_t[:, s:s + 1, :].to_broadcast([P, TILE_ROWS, JPAD]),
                                         mask_sb[:, :, :], ALU.mult).then_inc(diag_set, 1)
                    if q == 5:
                        gp.wait_ge(act_scaled, len(ACT_BANKS) * g + 2)
                        gp.tensor_tensor(pair[:, 0, :], pair[:, 0, :], pair[:, 1, :], ALU.add).then_inc(gp_steps, 1)
                    if q == 8:
                        gp.wait_ge(act_scaled, len(ACT_BANKS) * g + 3)
                        gp.wait_ge(gp_steps, GP_STEPS * g + 1)
                        gp.tensor_tensor(pair[:, 0, :], pair[:, 0, :], pair[:, 2, :], ALU.add).then_inc(gp_steps, 1)
                        gp.wait_ge(gp_steps, GP_STEPS * g + 2)
                        gp.tensor_tensor(pair[:, 0, 0:2 * H], pair[:, 0, 0:2 * H], pair[:, 0, 2 * H:4 * H],
                                         ALU.add).then_inc(gp_steps, 1)
                        gp.wait_ge(gp_steps, GP_STEPS * g + 3)
                        if s >= 2 or not first:
                            gp.wait_ge(dve_steps, DVE_STEPS * (g - 1))
                        gp.tensor_tensor(gp_sum[:, s % 2, :], pair[:, 0, 0:H], pair[:, 0, H:2 * H],
                                         ALU.add).then_inc(gp_steps, 1)
                    ahead, c, u = layer0_at(p)
                    if ahead == 0 or prepares:
                        layer0(k + ahead, c, u)
                    f, r = divmod(p - CHUNK_SLOTS - 1, 3)
                    if gathers and r == 0 and 0 <= f < F:
                        if f == 0:
                            gp.wait_ge(emb_turned, ETR * (k + 2))
                            gp.wait_ge(ids_in, 16 * (k + 3))
                            gp.nop(nofuse=True)
                        gather(f)

            gp.memset(x0[:, :].bitcast(F32), 0.0).then_inc(zeroed, 1)
            gp.wait_ge(ids_in, 16)
            for f in range(F):
                gather(f)
            gp.wait_ge(emb_turned, ETR)
            gp.wait_ge(ids_in, 16 * 2)
            for f in range(F):
                gather(f)
            for c in range(CHUNKS - 1):
                for u in range(CHUNK_SLOTS):
                    layer0(0, c, u)
            gp.wait_ge(consts_in, 16 * 5)
            gp.wait_ge(ones_set, 1)
            block_of(0, True, True, True)
            with gp.Fori(1, BLOCKS - 2) as k:
                block_of(k, False, True, True)
            block_of(BLOCKS - 2, False, True, False)
            block_of(BLOCKS - 1, False, False, False)

        @block.scalar
        def _(act):
            def turned(k, r):
                ps = ps_sel if r % 2 == 0 else ps_l2
                act.wait_ge(emb_turned, ETR * k + r + 1)
                act.activation(
                    x0[0:F, :].rearrange("p (b d) -> p d b", d=D)[:, 4 * r:4 * r + 4, :],
                    ps[0:F, :].rearrange("p (d b) -> p d b", d=4), ACT.Copy).then_inc(x0_hi_set, 1)

            def layer0(k, c, u):
                chunk = CHUNKS * k + c
                cols = slice(c * CHUNK, (c + 1) * CHUNK)
                known = isinstance(chunk, int)
                if u == 1:
                    act.wait_ge(copies_selected, chunk + 1)
                    if not (known and chunk == 0):
                        act.wait_ge(z_set, UNITS * chunk)
                        act.wait_ge(x0_turned, chunk)
                    act.activation(x0_copies[:, :], ps_sel[0:PAIRS, :], ACT.Copy).then_inc(copies_set, 1)
                if u == 4:
                    act.wait_ge(x0_turned, chunk + 1)
                    if not (known and chunk < CHUNKS):
                        act.wait_ge(dve_steps, DVE_STEPS * TPC * (chunk - CHUNKS + 1))
                        act.wait_ge(diag_set, TPC * (chunk - CHUNKS + 1))
                    act.activation(
                        x0_t[:, TPC * c:TPC * (c + 1), 0:F],
                        ps_x1[:, 0:TPC * JPAD].rearrange("p (t j) -> p t j", t=TPC)[:, :, 0:F],
                        ACT.Copy).then_inc(x0_t_set, 1)
                t, r = divmod(u - 6, 4)
                if r == 0 and 0 <= t < UNITS:
                    n = UNITS * chunk + t
                    b = (c * UNITS + t) % 2
                    act.wait_ge(z_set, n + 1)
                    if not (known and n < 2):
                        act.wait_ge(z_used, n - 1)
                        act.wait_ge(z_lo_set, n - 1)
                    act.activation(z_hi[:, b, :], z[:, b, :], ACT.Copy).then_inc(z_hi_set, 1)
                if u == 36:
                    act.wait_ge(z_used, UNITS * (chunk + 1))
                    if not (known and chunk < CHUNKS):
                        act.wait_ge(bank_done, BANKS * TPC * (chunk - CHUNKS + 1))
                    act.activation(x1_hi[:, cols], ps_x1[:, :], ACT.Identity,
                                   bias=b0_sb[:, 0:1]).then_inc(x1_hi_set, 1)

            def store_y(k, s):
                act.wait_ge(y_done, TILES * k + s + 1)
                act.activation(y_sb[:, :, TILE_ROWS * s:TILE_ROWS * (s + 1)],
                               ps_y[:, 0:TILE_ROWS * JPAD].rearrange("p (b j) -> p j b", j=JPAD),
                               ACT.Copy).then_inc(y_set, 1)

            def cin_features(k):
                act.wait_ge(l2_done, k + 1)
                act.activation(feat[:, 1, bass.ds(BLOCK_ROWS * k, BLOCK_ROWS)], y_sb[:, F, :],
                               ACT.Copy).then_inc(l1_feat_set, 1)
                act.activation(feat[:, 2, bass.ds(BLOCK_ROWS * k, BLOCK_ROWS)], ps_l2[:, 0:BLOCK_ROWS],
                               ACT.Identity, bias=b2_d[:, 0:1]).then_inc(l2_feat_set, 1)

            def block_of(k, first, prepares):
                for p in range(SLOTS):
                    s, q = divmod(p, BANKS)
                    g = TILES * k + s
                    if q in ACT_BANKS:
                        n = ACT_BANKS.index(q)
                        act.wait_ge(bank_done, BANKS * g + q + 1)
                        if n == 0 and (s >= 2 or not first):
                            act.wait_ge(gp_steps, GP_STEPS * (g - 1))
                        for x in range(JB):
                            j = JB * q + x
                            ins = act.activation(prod[:, s % 2, n, H * x:H * (x + 1)],
                                                 ps_t[(BANKS * s + q) % T_RING][:, H * x:H * (x + 1)],
                                                 ACT.Copy, scale=x0_t[:, s, j:j + 1])
                        ins.then_inc(act_scaled, 1)
                    if p == position(0, 9) and not first:
                        store_y(k - 1, TILES - 1)
                    if p == position(2, 5):
                        if not first:
                            cin_features(k - 1)
                            act.wait_ge(l1_feat_set, k)
                        store_y(k, 0)
                    if q == 9 and 2 <= s:
                        store_y(k, s - 1)
                    ahead, c, u = layer0_at(p)
                    if ahead == 0 or prepares:
                        layer0(k + ahead, c, u)
                    if prepares and p in TURN_AT:
                        turned(k + 1, TURN_AT.index(p))

            TURN_AT = [31, 33, 35, 37]
            act.wait_ge(w0_in, 16 * 3)
            act.activation(sel[:, :, :].rearrange("p t m -> p (t m)"), sel_raw, ACT.Copy).then_inc(sel_cast, 1)
            act.wait_ge(w0_folded, 1)
            act.activation(w0_hi[:, :, :].rearrange("p t h -> p (t h)"), w0_fwd_raw, ACT.Copy).then_inc(w0_split, 1)
            act.wait_ge(consts_in, 16 * 5)
            act.activation(b0_d[:, :], b0_sb[:, :], ACT.Copy, scale=float(D)).then_inc(bias_scaled, 1)
            act.activation(b2_d[:, :], b2_sb[:, :], ACT.Copy, scale=float(D)).then_inc(bias_scaled, 1)
            act.wait_ge(w1_in, 16)
            act.activation(w1_hi[:, :], w1_raw, ACT.Copy).then_inc(w1_hi_set, 1)
            act.wait_ge(bias_scaled, 2)
            act.wait_ge(zeroed, 1)
            for r in range(ETR):
                turned(0, r)
            for c in range(CHUNKS - 1):
                for u in range(CHUNK_SLOTS):
                    layer0(0, c, u)
            act.wait_ge(w1_split, 1)
            act.wait_ge(w0_split, 2)
            block_of(0, True, True)
            with act.Fori(1, BLOCKS - 1) as k:
                block_of(k, False, True)
            block_of(BLOCKS - 1, False, False)
            store_y(BLOCKS - 1, TILES - 1)
            cin_features(BLOCKS - 1)
            for half in range(2):
                for m in range(TOP1 // P):
                    act.wait_ge(top_mm, 7 * half + m + 1)
                    if m == 0 and half == 1:
                        act.wait_ge(top_mm, 6)
                    act.activation(h1[:, m, :], ps_t[m][:, :], ACT.Relu, bias=bt1[:, m:m + 1]).then_inc(top_act, 1)
                for m in range(TOP2 // P):
                    act.wait_ge(top_mm, 7 * half + 5 + m)
                    act.activation(h2[:, m, :], (ps_sel, ps_x1)[m][:, :], ACT.Relu,
                                   bias=bt2[:, m:m + 1]).then_inc(top_act, 1)
                act.wait_ge(top_mm, 7 * half + 7)
                act.activation(y_out[:, 512 * half:512 * half + 512], ps_y[0:1, :], ACT.Copy).then_inc(top_act, 1)

        @block.vector
        def _(dve):
            def turned(k, r):
                ps = ps_sel if r % 2 == 0 else ps_l2
                dve.wait_ge(x0_hi_set, ETR * k + r + 1)
                dve.tensor_tensor(
                    x0[LO:SPLIT, :].rearrange("p (b d) -> p d b", d=D)[:, 4 * r:4 * r + 4, :],
                    ps[0:F, :].rearrange("p (d b) -> p d b", d=4),
                    x0[0:F, :].bitcast(F32).rearrange("p (b d) -> p d b", d=D)[:, 4 * r:4 * r + 4, :],
                    ALU.subtract).then_inc(x0_lo_set, 1)

            def layer0(k, c, u):
                chunk = CHUNKS * k + c
                cols = slice(c * CHUNK, (c + 1) * CHUNK)
                known = isinstance(chunk, int)
                t, r = divmod(u - 5, 4)
                if r == 0 and 0 <= t < UNITS:
                    n = UNITS * chunk + t
                    b = (c * UNITS + t) % 2
                    if t == 0:
                        dve.wait_ge(copies_set, chunk + 1)
                    dve.wait_ge(shift_selected, n + 1)
                    if not (known and n < 2):
                        dve.wait_ge(z_lo_set, n - 1)
                    dve.tensor_tensor(z[:, b, :], ps_sel[0:PAIRS, :], x0_copies[:, :], ALU.mult).then_inc(z_set, 1)
                if u == 37:
                    dve.wait_ge(x1_hi_set, chunk + 1)
                    dve.scalar_tensor_tensor(x1_lo[:, cols], ps_x1[:, :], b0_sb[:, 0:1], x1_hi[:, cols].bitcast(F32),
                                             ALU.add, ALU.subtract).then_inc(x1_done, 1)
                    dve.tensor_reduce(feat[:, 0, bass.ds(BLOCK_ROWS * k + CHUNK // D * c, CHUNK // D)],
                                      ps_x1[:, :].rearrange("p (b d) -> p b d", d=D), AX.X,
                                      ALU.add).then_inc(x1_done, 1)

            def join(k, s, first):
                g = TILES * k + s
                dve.wait_ge(dve_steps, DVE_STEPS * g + DVE_UNITS)
                dve.tensor_tensor(dve_sum[:, s % 2, 0, :], dve_sum[:, s % 2, 0, :], dve_sum[:, s % 2, 1, :],
                                  ALU.add).then_inc(dve_steps, 1)
                dve.wait_ge(gp_steps, GP_STEPS * (g + 1))
                dve.wait_ge(dve_steps, DVE_STEPS * g + DVE_UNITS + 1)
                if not (first and s < 4):
                    dve.wait_ge(y_done, g - 3)
                dve.tensor_tensor(x2[:, s % 4, :], dve_sum[:, s % 2, 0, :], gp_sum[:, s % 2, :],
                                  ALU.add).then_inc(dve_steps, 1)

            def block_of(k, first, prepares):
                for p in range(SLOTS):
                    s, q = divmod(p, BANKS)
                    g = TILES * k + s
                    if q in DVE_BANKS:
                        dve.wait_ge(bank_done, BANKS * g + q + 1)
                        if q == 0 and s % TPC == 0:
                            dve.wait_ge(x0_t_set, CHUNKS * k + s // TPC + 1)
                        for x in range(FIELDS_OF[q]):
                            n = dve_units_before(q) + x
                            j = JB * q + x
                            mine = dve_sum[:, s % 2, n % 2, :]
                            t_j = ps_t[(BANKS * s + q) % T_RING][:, H * x:H * (x + 1)]
                            if n >= 2:
                                dve.wait_ge(dve_steps, DVE_STEPS * g + n - 1)
                            if n == 1:
                                dve.tensor_scalar(mine, t_j, x0_t[:, s, j:j + 1], None, ALU.mult).then_inc(dve_steps, 1)
                            else:
                                dve.scalar_tensor_tensor(mine, t_j, x0_t[:, s, j:j + 1], b1_sb[:, :] if n == 0 else mine,
                                                         ALU.mult, ALU.add).then_inc(dve_steps, 1)
                    if q == BANKS - 1:
                        join(k, s, first)
                    ahead, c, u = layer0_at(p)
                    if ahead == 0 or prepares:
                        layer0(k + ahead, c, u)
                    if prepares and p in TURN_AT:
                        turned(k + 1, TURN_AT.index(p))

            TURN_AT = [32, 34, 36, 38]
            dve.memset(x0_t[:, :, F:JPAD], 1.0).then_inc(ones_set, 1)
            dve.wait_ge(w0_in, 16 * 3)
            dve.tensor_tensor(w0_fwd_raw, w0_fwd_raw, w0_rev_raw, ALU.add).then_inc(w0_folded, 1)
            dve.wait_ge(w0_split, 1)
            dve.tensor_tensor(w0_lo[:, :, :].rearrange("p t h -> p (t h)"), w0_fwd_raw,
                              w0_hi[:, :, :].rearrange("p t h -> p (t h)").bitcast(F32),
                              ALU.subtract).then_inc(w0_split, 1)
            dve.wait_ge(w1_hi_set, 1)
            dve.tensor_tensor(w1_lo[:, :], w1_raw, w1_hi[:, :].bitcast(F32), ALU.subtract).then_inc(w1_split, 1)
            dve.wait_ge(consts_in, 16 * 5)
            for r in range(ETR):
                turned(0, r)
            for c in range(CHUNKS - 1):
                for u in range(CHUNK_SLOTS):
                    layer0(0, c, u)
            block_of(0, True, True)
            with dve.Fori(1, BLOCKS - 1) as k:
                block_of(k, False, True)
            block_of(BLOCKS - 1, False, False)
            dve.wait_ge(x1_done, 2 * CHUNKS * BLOCKS)
            dve.wait_ge(bias_scaled, 2)
            dve.tensor_scalar(feat[:, 0, :], feat[:, 0, :], b0_d[:, 0:1], None, ALU.add).then_inc(feat0_done, 1)

        @block.tensor
        def _(pe):
            def turn(k, r):
                ps = ps_sel if r % 2 == 0 else ps_l2
                known = isinstance(k, int)
                if r == 0:
                    pe.wait_ge(emb_in, 16 * F * (k + 1))
                    if not (known and k == 0):
                        pe.wait_ge(z_set, UNITS * CHUNKS * k)
                if r == 1 and not (known and k < 2):
                    pe.wait_ge(l2_feat_set, k - 1)
                if r >= 2:
                    pe.wait_ge(x0_lo_set, ETR * k + r - 1)
                pe.nop(nofuse=True)
                for x in range(4):
                    ins = pe.transpose(ps[0:F, BLOCK_ROWS * x:BLOCK_ROWS * (x + 1)],
                                       emb[:, :].rearrange("p (j d) -> p d j", d=D)[:, 4 * r + x, :],
                                       ident_sb[:, :])
                ins.then_inc(emb_turned, 1)

            def layer0(k, c, u):
                chunk = CHUNKS * k + c
                known = isinstance(chunk, int)
                cols = slice(c * CHUNK, (c + 1) * CHUNK)
                if u == 0:
                    pe.wait_ge(x0_lo_set, ETR * (k + 1))
                    if not (known and chunk == 0):
                        pe.wait_ge(z_set, UNITS * chunk)
                    pe.matmul(ps_sel[0:PAIRS, :], sel[:, UNITS, :], x0[:, cols], start=True,
                              stop=True).then_inc(copies_selected, 1)
                if u == 3:
                    pe.wait_ge(copies_set, chunk + 1)
                    if not (known and chunk == 0):
                        pe.wait_ge(x1_done, 2 * chunk)
                    pe.nop(nofuse=True)
                    for t in range(TPC):
                        ins = pe.transpose(ps_x1[:, JPAD * t:JPAD * t + F], x0_copies[0:F, P * t:P * (t + 1)],
                                           ident_sb[0:F, 0:F])
                    ins.then_inc(x0_turned, 1)
                t, r = divmod(u - 4, 4)
                if r == 0 and 0 <= t < UNITS:
                    n = UNITS * chunk + t
                    if t == 0:
                        pe.wait_ge(copies_set, chunk + 1)
                    else:
                        pe.wait_ge(z_set, n)
                    pe.matmul(ps_sel[0:PAIRS, :], sel[:, t, :], x0[:, cols], start=True,
                              stop=True).then_inc(shift_selected, 1)
                t, r = divmod(u - 11, 4)
                if r == 0 and 0 <= t < UNITS:
                    n = UNITS * chunk + t
                    b = (c * UNITS + t) % 2
                    if t == 0:
                        pe.wait_ge(x0_t_set, chunk + 1)
                    pe.wait_ge(z_lo_set, n + 1)
                    pe.matmul(ps_x1[:, :], w0_hi[:, t, :], z_hi[:, b, :], start=(t == 0), stop=False)
                    pe.matmul(ps_x1[:, :], w0_lo[:, t, :], z_hi[:, b, :], start=False, stop=False)
                    pe.matmul(ps_x1[:, :], w0_hi[:, t, :], z_lo[:, b, :], start=False,
                              stop=(t == UNITS - 1)).then_inc(z_used, 1)

            def sum_over_d(k, s):
                g = TILES * k + s
                pe.wait_ge(dve_steps, DVE_STEPS * (g + 1))
                pe.wait_ge(diag_set, g + 1)
                if not (isinstance(g, int) and g == 0):
                    pe.wait_ge(y_set, g)
                pe.matmul(ps_y[:, 0:TILE_ROWS * JPAD], x2[:, s % 4, :],
                          x0_diag[:, s % 4].rearrange("p b j -> p (b j)"), start=True, stop=True).then_inc(y_done, 1)

            def layer2(k, j):
                if j == 0:
                    pe.wait_ge(y_set, TILES * (k + 1))
                    if not (isinstance(k, int) and k == BLOCKS - 1):
                        pe.wait_ge(x0_lo_set, ETR * (k + 2))
                ins = pe.matmul(ps_l2[:, 0:BLOCK_ROWS], w2_sb[:, j, :], y_sb[:, j, :], start=(j == 0), stop=(j == F - 1))
                if j == F - 1:
                    ins.then_inc(l2_done, 1)

            def block_of(k, first, prepares):
                for p in range(SLOTS):
                    s, q = divmod(p, BANKS)
                    g = TILES * k + s
                    if not (first and p < T_RING):
                        so, qo = divmod(p - T_RING, BANKS)
                        go = TILES * k + so
                        if qo in ACT_BANKS:
                            pe.wait_ge(act_scaled, len(ACT_BANKS) * go + act_banks_before(qo) + 1)
                        else:
                            pe.wait_ge(dve_steps, DVE_STEPS * go + dve_units_before(qo + 1))
                    if q == 0 and s % TPC == 0:
                        pe.wait_ge(x1_done, 2 * (CHUNKS * k + s // TPC + 1))
                    w = FIELDS_OF[q] * H
                    ps = ps_t[p % T_RING][:, 0:w]
                    cols = slice(P * s, P * (s + 1))
                    js = slice(JB * H * q, JB * H * q + w)
                    pe.matmul(ps, x1_hi[:, cols], w1_hi[:, js], start=True, stop=False)
                    pe.matmul(ps, x1_hi[:, cols], w1_lo[:, js], start=False, stop=False)
                    pe.matmul(ps, x1_lo[:, cols], w1_hi[:, js], start=False, stop=True).then_inc(bank_done, 1)
                    if p == position(0, 8) and not first:
                        sum_over_d(k - 1, TILES - 1)
                    if not first and L2_FROM <= p < L2_FROM + L2_SLOTS:
                        for j in range(L2_EACH * (p - L2_FROM), min(F, L2_EACH * (p - L2_FROM + 1))):
                            layer2(k - 1, j)
                    if p == position(2, 5):
                        sum_over_d(k, 0)
                    if q == 8 and s >= 2:
                        sum_over_d(k, s - 1)
                    ahead, c, u = layer0_at(p)
                    if ahead == 0 or prepares:
                        layer0(k + ahead, c, u)
                    if prepares and p in TURN_AT:
                        turn(k + 1, TURN_AT.index(p))

            TURN_AT = [30, 32, 34, 36]
            pe.wait_ge(consts_in, 16 * 5)
            for r in range(ETR):
                turn(0, r)
            pe.wait_ge(sel_cast, 1)
            pe.wait_ge(w0_split, 2)
            for c in range(CHUNKS - 1):
                for u in range(CHUNK_SLOTS):
                    layer0(0, c, u)
            pe.wait_ge(w1_split, 1)
            block_of(0, True, True)
            pe.wait_ge(w2_in, 16)
            with pe.Fori(1, BLOCKS - 1) as k:
                block_of(k, False, True)
            block_of(BLOCKS - 1, False, False)
            sum_over_d(BLOCKS - 1, TILES - 1)
            for j in range(F):
                layer2(BLOCKS - 1, j)
            pe.wait_ge(top_in, 16 * 7)
            pe.wait_ge(feat0_done, 1)
            pe.wait_ge(l2_feat_set, BLOCKS)
            for half in range(2):
                rows = slice(512 * half, 512 * half + 512)
                for m in range(TOP1 // P):
                    if half == 0:
                        pe.wait_ge(dve_steps, DVE_STEPS * TILES * BLOCKS)
                        pe.wait_ge(act_scaled, len(ACT_BANKS) * TILES * BLOCKS)
                    else:
                        pe.wait_ge(top_act, m + 1)
                    for n in range(N_CIN):
                        pe.matmul(ps_t[m][:, :], wt1[:, n, P * m:P * (m + 1)], feat[:, n, rows], start=(n == 0), stop=False)
                    pe.matmul(ps_t[m][:, :], wt1_dense[:, P * m:P * (m + 1)], dense[:, rows], start=False,
                              stop=True).then_inc(top_mm, 1)
                for m in range(TOP2 // P):
                    pe.wait_ge(top_act, 7 * half + TOP1 // P)
                    for n in range(TOP1 // P):
                        ins = pe.matmul((ps_sel, ps_x1)[m][:, :], wt2[:, n, P * m:P * (m + 1)], h1[:, n, :],
                                        start=(n == 0), stop=(n == TOP1 // P - 1))
                    ins.then_inc(top_mm, 1)
                pe.wait_ge(top_act, 7 * half + 6)
                for n in range(TOP2 // P):
                    ins = pe.matmul(ps_y[0:1, :], wt3[:, n:n + 1], h2[:, n, :], start=(n == 0), stop=(n == TOP2 // P - 1))
                ins.then_inc(top_mm, 1)


def _pair_layout(w, reverse):
    import numpy as np
    o = np.zeros((COPIES, F, UNITS, H), w.dtype)
    j = np.arange(F)
    for t in range(UNITS):
        for g in range(COPIES):
            s = COPIES * t + g
            if s > F // 2 or (reverse and s == 0):
                continue
            k = (j + s) % F
            o[g, :, t, :] = (w[:, k, j] if reverse else w[:, j, k]).T
    return o.reshape(PAIRS, UNITS * H)


def _select_layout():
    import numpy as np
    o = np.zeros((SPLIT, UNITS + 1, COPIES, F), np.float32)
    for t in range(UNITS + 1):
        for g in range(COPIES):
            s = 0 if t == UNITS else COPIES * t + g
            for j in range(F):
                o[(j + s) % F, t, g, j] = 1.0
                o[LO + (j + s) % F, t, g, j] = 1.0
    return o.reshape(SPLIT, (UNITS + 1) * PAIRS)


def kernel(**inputs):
    import numpy as np
    import concourse.bacc as _bacc
    from concourse import mybir as _mybir
    from concourse.bass_utils import run_bass_kernel_spmd as _run

    a = {n: np.asarray(v) for n, v in inputs.items()}
    mask = np.zeros((P, TILE_ROWS, JPAD), np.float32)
    for p in range(P):
        mask[p, p // D, :] = 1.0
    arrays = {
        "ids": a["ids"].reshape(BLOCKS, BLOCK_ROWS, F),
        "dense_t": a["dense_ctx"].T,
        "w0_fwd": _pair_layout(a["L0_rec_W0"].reshape(H, F, F), False),
        "w0_rev": _pair_layout(a["L0_rec_W0"].reshape(H, F, F), True),
        "w1": a["L0_rec_W1"].reshape(H, F, H).transpose(2, 1, 0).reshape(H, F * H),
        "w2": a["L0_rec_W2"].reshape(H, F, H).transpose(2, 1, 0),
        "b0": a["L0_rec_b0"].reshape(H, 1),
        "b1_rows": np.broadcast_to(a["L0_rec_b1"], (P, H)),
        "b2": a["L0_rec_b2"].reshape(H, 1),
        "select": _select_layout(),
        "ident": np.eye(P, dtype=np.float32),
        "mask": mask,
        "w_top1": a["W_top1"][:N_CIN * H].reshape(N_CIN, H, TOP1).transpose(1, 0, 2),
        "w_top1_dense": a["W_top1"][N_CIN * H:],
        "b_top1": a["b_top1"].reshape(TOP1 // P, P).T,
        "w_top2": a["W_top2"].reshape(TOP1 // P, P, TOP2).transpose(1, 0, 2),
        "b_top2": a["b_top2"].reshape(TOP2 // P, P).T,
        "w_top3": a["W_top3"].reshape(TOP2 // P, P).T,
    }
    for f in range(F):
        arrays[f"tbl_{f}"] = a[f"tbl_{f}"]
    nc = _bacc.Bacc("TRN2", target_bir_lowering=False, num_devices=1)
    args, maps = {}, {}
    for n, v in arrays.items():
        v = np.ascontiguousarray(v)
        maps[f"in_{n}"] = v
        args[n] = nc.dram_tensor(f"in_{n}", v.shape, _mybir.dt.from_np(v.dtype), kind="ExternalInput").ap()
    tables = [args.pop(f"tbl_{f}") for f in range(F)]
    out = nc.dram_tensor("out_0", (B, 1), _mybir.dt.float32, kind="ExternalOutput").ap()
    cin_tower(nc, **args, out=out, tables=tables)
    return _run(nc, [maps], core_ids=[0]).results[0]["out_0"]
```

```python
from contextlib import ExitStack

import concourse.bass as bass
from concourse import mybir

F32 = mybir.dt.float32
F32R = mybir.dt.float32r
I32 = mybir.dt.int32
ALU = mybir.AluOpType
ACT = mybir.ActivationFunctionType
AX = mybir.AxisListType

P = 128
B, F, D, H = 1024, 39, 16, 128
N_CIN = 3
DENSE = 16
TOP1, TOP2 = 512, 256
BLOCK_ROWS = 128
BLOCKS = B // BLOCK_ROWS
BLOCK_COLS = BLOCK_ROWS * D
CHUNKS = 4
CHUNK = BLOCK_COLS // CHUNKS
TILES = BLOCK_COLS // P
TPC = TILES // CHUNKS
TILE_ROWS = P // D
COPIES = 3
PAIRS = COPIES * F
UNITS = -(-(F // 2 + 1) // COPIES)
LO = 64
SPLIT = LO + F
JB = 4
BANKS = -(-F // JB)
T_RING = 4
Z_RING = 4
JOIN_AT = (2, 3)
J1 = F + 1
JPAD = 40

ACT_BANKS = (0, 2, 4, 7)
FIELDS_OF = [min(JB, F - JB * q) for q in range(BANKS)]
DVE_BANKS = tuple(q for q in range(BANKS) if q not in ACT_BANKS)
DVE_UNITS = sum(FIELDS_OF[q] for q in DVE_BANKS)
GP_STEPS = len(ACT_BANKS)
DVE_LOW = tuple(range(1, UNITS, 2))
DIAG_RING = 2 * TPC
ETR = 4
L2_FROM, L2_SLOTS, L2_EACH = 11, 13, 3
SLOTS = TILES * BANKS
CHUNK_SLOTS = TPC * BANKS
STEP = 3
SELECT_AT, Z_AT, Z_HI_AT, Z_LO_AT, SUM_AT = 2, 4, 7, 8, 14
COPIES_AT, X0_TURN_AT, X0_T_AT, X1_HI_AT, X1_LO_AT = 1, 3, 5, 33, 34
TURN_AT = [2 * CHUNK_SLOTS + x for x in (25, 28, 31, 34)]
GATHER_FROM, GATHER_STEP = 3 * CHUNK_SLOTS + 1, 3
GATHERS_FIRST = -(-(SLOTS - GATHER_FROM) // GATHER_STEP)


def dve_units_before(q):
    return sum(FIELDS_OF[x] for x in DVE_BANKS if x < q)


def low_part_count(chunk, t):
    return (UNITS // 2 if t in DVE_LOW else UNITS - UNITS // 2) * chunk + t // 2 + 1


def act_banks_before(q):
    return sum(1 for x in ACT_BANKS if x < q)


def cin_tower(nc, ids, dense_t, w0_fwd, w0_rev, w1, w2, b0, b1_rows, b2, select, ident, mask,
              w_top1, w_top1_dense, b_top1, w_top2, b_top2, w_top3, out, tables):
    with ExitStack() as ctx:
        def sb(name, shape, dt=F32):
            return ctx.enter_context(nc.sbuf_tensor(name, shape, dt))

        def bank(name):
            return ctx.enter_context(nc.psum_tensor(name, [P, 512], F32))

        def sem(name):
            return ctx.enter_context(nc.semaphore(name))

        w1_hi = sb("w1_hi", [P, F * H], F32R)
        w1_lo = sb("w1_lo", [P, F * H], F32R)
        w2_sb = sb("w2_sb", [P, F, H])
        w0_hi = sb("w0_hi", [PAIRS, UNITS, H], F32R)
        w0_lo = sb("w0_lo", [PAIRS, UNITS, H], F32R)
        sel = sb("sel", [SPLIT, UNITS + 1, PAIRS], F32R)
        ident_sb = sb("ident_sb", [P, P])
        b0_sb = sb("b0_sb", [P, 1])
        b1_sb = sb("b1_sb", [P, H])
        b2_sb = sb("b2_sb", [P, 1])
        b0_d = sb("b0_d", [P, 1])
        b2_d = sb("b2_d", [P, 1])
        wt1 = sb("wt1", [P, N_CIN, TOP1])
        wt1_dense = sb("wt1_dense", [DENSE, TOP1])
        wt2 = sb("wt2", [P, TOP1 // P, TOP2])
        wt3 = sb("wt3", [P, TOP2 // P])
        bt1 = sb("bt1", [P, TOP1 // P])
        bt2 = sb("bt2", [P, TOP2 // P])
        ids_cur = sb("ids_cur", [P, F], I32)
        emb = sb("emb", [P, F * D])
        x0 = sb("x0", [SPLIT, BLOCK_COLS], F32R)
        x0_copies = sb("x0_copies", [PAIRS, CHUNK])
        x0_t = sb("x0_t", [P, TILES, JPAD])
        z = sb("z", [PAIRS, Z_RING, CHUNK])
        z_hi = sb("z_hi", [PAIRS, Z_RING, CHUNK], F32R)
        z_lo = sb("z_lo", [PAIRS, Z_RING, CHUNK], F32R)
        x1_hi = sb("x1_hi", [P, BLOCK_COLS], F32R)
        x1_lo = sb("x1_lo", [P, BLOCK_COLS], F32R)
        prod = sb("prod", [P, 2, len(ACT_BANKS), JB * H])
        gp_sum = sb("gp_sum", [P, 2, 2, H])
        dve_sum = sb("dve_sum", [P, 2, 2, H])
        x2 = sb("x2", [P, 4, H])
        x0_diag = sb("x0_diag", [P, DIAG_RING, TILE_ROWS, JPAD])
        y_sb = sb("y_sb", [P, JPAD, BLOCK_ROWS])
        feat = sb("feat", [P, N_CIN, B])
        dense = sb("dense", [DENSE, B])
        w2_flat = w2_sb[:, :, :].rearrange("p j h -> p (j h)")
        h1 = w2_flat[:, 0:4 * 512].rearrange("p (m n) -> p m n", m=TOP1 // P)
        h2 = w2_flat[:, 4 * 512:6 * 512].rearrange("p (m n) -> p m n", m=TOP2 // P)
        y_out = w2_flat[0:1, 6 * 512:6 * 512 + B]
        w1_raw = y_sb[:, 0:F, :].rearrange("p j h -> p (j h)")
        raw = prod[:, :, :, :].rearrange("p a b c -> p (a b c)")
        n_w0 = UNITS * H
        w0_fwd_raw = raw[0:PAIRS, 0:n_w0]
        w0_rev_raw = raw[0:PAIRS, n_w0:2 * n_w0]
        sel_raw = raw[0:SPLIT, 2 * n_w0:2 * n_w0 + (UNITS + 1) * PAIRS]

        ps_t = [bank(f"ps_t{i}") for i in range(T_RING)]
        ps_sel = [bank(f"ps_sel{i}") for i in range(2)]
        ps_x1 = bank("ps_x1")
        ps_y = bank("ps_y")

        consts_in = sem("consts_in")
        mask_in = sem("mask_in")
        w0_in = sem("w0_in")
        w1_in = sem("w1_in")
        w2_in = sem("w2_in")
        top_in = sem("top_in")
        ids_in = sem("ids_in")
        emb_in = sem("emb_in")
        out_done = sem("out_done")
        zeroed = sem("zeroed")
        w0_folded = sem("w0_folded")
        w0_split = sem("w0_split")
        sel_cast = sem("sel_cast")
        w1_hi_set = sem("w1_hi_set")
        w1_split = sem("w1_split")
        bias_scaled = sem("bias_scaled")
        emb_turned = sem("emb_turned")
        x0_hi_set = sem("x0_hi_set")
        x0_lo_set = sem("x0_lo_set")
        copies_selected = sem("copies_selected")
        copies_set = sem("copies_set")
        x0_turned = sem("x0_turned")
        x0_t_set = sem("x0_t_set")
        shift_selected = sem("shift_selected")
        z_set = sem("z_set")
        z_hi_set = sem("z_hi_set")
        z_lo_gp = sem("z_lo_gp")
        z_lo_dve = sem("z_lo_dve")
        z_used = sem("z_used")
        x1_hi_set = sem("x1_hi_set")
        x1_done = sem("x1_done")
        bank_done = sem("bank_done")
        dve_steps = sem("dve_steps")
        act_scaled = sem("act_scaled")
        gp_steps = sem("gp_steps")
        joined = sem("joined")
        diag_in = [sem(f"diag_in{i}") for i in range(2)]
        y_done = sem("y_done")
        y_set = sem("y_set")
        l2_done = sem("l2_done")
        l1_feat_set = sem("l1_feat_set")
        l2_feat_set = sem("l2_feat_set")
        feat0_done = sem("feat0_done")
        top_mm = sem("top_mm")
        top_act = sem("top_act")

        block = ctx.enter_context(nc.Block())

        def z_lo_set(t):
            return z_lo_dve if t in DVE_LOW else z_lo_gp

        def ring_before(chunk, t):
            return (chunk, t - Z_RING) if t >= Z_RING else (chunk - 1, t - Z_RING + UNITS)

        def position(s, q):
            return s * BANKS + q

        def layer0_at(p):
            c = p // CHUNK_SLOTS + 1
            return c // CHUNKS, c % CHUNKS, p % CHUNK_SLOTS

        @block.sync
        def _(sp):
            sp.dma_start(ids_cur[:, :], ids[0]).then_inc(ids_in, 16)
            sp.dma_start(ident_sb[:, :], ident).then_inc(consts_in, 16)
            for i in range(DIAG_RING):
                sp.dma_start(x0_diag[:, i], mask).then_inc(mask_in, 16)
            sp.dma_start(b0_sb[:, :], b0).then_inc(consts_in, 16)
            sp.dma_start(b1_sb[:, :], b1_rows).then_inc(consts_in, 16)
            sp.dma_start(b2_sb[:, :], b2).then_inc(consts_in, 16)
            sp.dma_start(sel_raw, select).then_inc(w0_in, 16)
            sp.dma_start(w0_fwd_raw, w0_fwd).then_inc(w0_in, 16)
            sp.dma_start(w0_rev_raw, w0_rev).then_inc(w0_in, 16)
            sp.dma_start(w1_raw, w1).then_inc(w1_in, 16)
            sp.dma_start(w2_sb[:, :, :], w2).then_inc(w2_in, 16)
            for t, d in ((wt1[:, :, :], w_top1), (wt1_dense[:, :], w_top1_dense), (bt1[:, :], b_top1),
                         (wt2[:, :, :], w_top2), (bt2[:, :], b_top2), (wt3[:, :], w_top3),
                         (dense[:, :], dense_t)):
                sp.dma_start(t, d).then_inc(top_in, 16)

            def next_ids(k):
                sp.wait_ge(emb_in, 16 * F * k)
                src = ids[k] if isinstance(k, int) else ids[bass.ds(k, 1)].rearrange("a p f -> (a p) f")
                sp.dma_start(ids_cur[:, :], src).then_inc(ids_in, 16)

            def diagonal(k, c):
                chunk = CHUNKS * k + c
                sp.wait_ge(x0_t_set, chunk + 1)
                sp.nop(nofuse=True)
                if not (isinstance(chunk, int) and chunk < 2):
                    sp.wait_ge(y_done, TPC * (chunk - 1))
                for r in range(TILE_ROWS):
                    rows = slice(D * r, D * r + D)
                    sp.dma_start(x0_diag[rows, TPC * (c % 2):TPC * (c % 2 + 1), r, 0:F],
                                 x0_t[rows, TPC * c:TPC * (c + 1), 0:F]).then_inc(diag_in[c % 2], 16)

            next_ids(1)
            sp.wait_ge(mask_in, 16 * DIAG_RING)
            diagonal(0, 0)
            for c in range(1, CHUNKS):
                diagonal(0, c)
            next_ids(2)
            diagonal(1, 0)
            with sp.Fori(1, BLOCKS - 2) as k:
                for c in range(1, CHUNKS):
                    diagonal(k, c)
                next_ids(k + 2)
                diagonal(k + 1, 0)
            for c in range(1, CHUNKS):
                diagonal(BLOCKS - 2, c)
            for c in range(CHUNKS):
                diagonal(BLOCKS - 1, c)
            sp.wait_ge(top_act, 2 * 7)
            sp.dma_start(out.rearrange("b a -> a b"), y_out[:, :]).then_inc(out_done, 16)
            sp.wait_ge(out_done, 16)

        @block.gpsimd
        def _(gp):
            def gather(f):
                gp.indirect_dma_start(emb[:, D * f:D * f + D], None, tables[f],
                                      bass.IndirectOffsetOnAxis(ap=ids_cur[:, f:f + 1], axis=0)).then_inc(emb_in, 16)

            def layer0(k, c, u):
                t, r = divmod(u - Z_LO_AT, STEP)
                if r == 0 and 0 <= t < UNITS and t not in DVE_LOW:
                    n = (k * CHUNKS + c) * UNITS + t
                    b = (c * UNITS + t) % Z_RING
                    gp.wait_ge(z_hi_set, n + 1)
                    if not (isinstance(n, int) and n < Z_RING):
                        gp.wait_ge(z_used, n - Z_RING + 1)
                    gp.tensor_tensor(z_lo[:, b, :], z[:, b, :], z_hi[:, b, :].bitcast(F32),
                                     ALU.subtract).then_inc(z_lo_gp, 1)

            def block_of(k, first, prepares, gathers):
                for p in range(SLOTS):
                    s, q = divmod(p, BANKS)
                    g = TILES * k + s
                    pair = prod[:, s % 2]
                    if q - 1 in ACT_BANKS[1:]:
                        n = ACT_BANKS.index(q - 1)
                        if n >= 2:
                            gp.wait_ge(gp_steps, GP_STEPS * g + n - 1)
                        gp.wait_ge(act_scaled, len(ACT_BANKS) * g + n + 1)
                        gp.tensor_tensor(pair[:, 0, :], pair[:, 0, :], pair[:, n, :], ALU.add).then_inc(gp_steps, 1)
                        if n == len(ACT_BANKS) - 1:
                            gp.wait_ge(gp_steps, GP_STEPS * g + n)
                            if s >= 2 or not first:
                                gp.wait_ge(joined, 2 * (g - 1))
                            gp.tensor_tensor(gp_sum[:, s % 2].rearrange("p a h -> p (a h)"), pair[:, 0, 0:2 * H],
                                             pair[:, 0, 2 * H:4 * H], ALU.add).then_inc(gp_steps, 1)
                    ahead, c, u = layer0_at(p)
                    if ahead == 0 or prepares:
                        layer0(k + ahead, c, u)
                    f, r = divmod(p - GATHER_FROM, GATHER_STEP)
                    if gathers and r == 0 and f >= 0:
                        if f == 0:
                            gp.wait_ge(emb_turned, ETR * (k + 2))
                            gp.wait_ge(ids_in, 16 * (k + 3))
                            gp.nop(nofuse=True)
                        gather(f)
                    f, r = divmod(p, GATHER_STEP)
                    if prepares and r == 0 and f + GATHERS_FIRST < F:
                        if f == 0:
                            gp.nop(nofuse=True)
                        gather(f + GATHERS_FIRST)

            gp.memset(x0[:, :].bitcast(F32), 0.0).then_inc(zeroed, 1)
            gp.wait_ge(ids_in, 16)
            for f in range(F):
                gather(f)
            for u in range(CHUNK_SLOTS):
                layer0(0, 0, u)
            gp.wait_ge(emb_turned, ETR)
            gp.wait_ge(ids_in, 16 * 2)
            for f in range(GATHERS_FIRST):
                gather(f)
            block_of(0, True, True, True)
            with gp.Fori(1, BLOCKS - 2) as k:
                block_of(k, False, True, True)
            block_of(BLOCKS - 2, False, True, False)
            block_of(BLOCKS - 1, False, False, False)

        @block.scalar
        def _(act):
            def turned(k, r):
                ps = ps_sel[r % 2]
                act.wait_ge(emb_turned, ETR * k + r + 1)
                if r == 0 and not (isinstance(k, int) and k == 0):
                    act.wait_ge(shift_selected, UNITS * CHUNKS * k)
                act.activation(
                    x0[0:F, :].rearrange("p (b d) -> p d b", d=D)[:, 4 * r:4 * r + 4, :],
                    ps[0:F, :].rearrange("p (d b) -> p d b", d=4), ACT.Copy).then_inc(x0_hi_set, 1)

            def layer0(k, c, u):
                chunk = CHUNKS * k + c
                cols = slice(c * CHUNK, (c + 1) * CHUNK)
                known = isinstance(chunk, int)
                if u == COPIES_AT:
                    act.wait_ge(copies_selected, chunk + 1)
                    if not (known and chunk == 0):
                        act.wait_ge(z_set, UNITS * chunk)
                        act.wait_ge(x0_turned, chunk)
                    act.activation(x0_copies[:, :], ps_sel[0][0:PAIRS, :], ACT.Copy).then_inc(copies_set, 1)
                if u == X0_T_AT:
                    act.wait_ge(x0_turned, chunk + 1)
                    if not (known and chunk < CHUNKS):
                        act.wait_ge(dve_steps, DVE_UNITS * TPC * (chunk - CHUNKS + 1))
                        act.wait_ge(diag_in[c % 2], 16 * TILE_ROWS * (2 * k + c // 2 - 1))
                    act.activation(
                        x0_t[:, TPC * c:TPC * (c + 1), 0:F],
                        ps_x1[:, :].rearrange("p (t j) -> p t j", t=TPC)[:, :, 0:F],
                        ACT.Copy).then_inc(x0_t_set, 1)
                t, r = divmod(u - Z_HI_AT, STEP)
                if r == 0 and 0 <= t < UNITS:
                    n = UNITS * chunk + t
                    b = (c * UNITS + t) % Z_RING
                    act.wait_ge(z_set, n + 1)
                    if not (known and n < Z_RING):
                        act.wait_ge(z_used, n - Z_RING + 1)
                        was, tw = ring_before(chunk, t)
                        act.wait_ge(z_lo_set(tw), low_part_count(was, tw))
                    act.activation(z_hi[:, b, :], z[:, b, :], ACT.Copy).then_inc(z_hi_set, 1)
                if u == X1_HI_AT:
                    act.wait_ge(z_used, UNITS * (chunk + 1))
                    if not (known and chunk < CHUNKS):
                        act.wait_ge(bank_done, BANKS * TPC * (chunk - CHUNKS + 1))
                    act.activation(x1_hi[:, cols], ps_x1[:, :], ACT.Identity,
                                   bias=b0_sb[:, 0:1]).then_inc(x1_hi_set, 1)

            def store_y(k, s):
                act.wait_ge(y_done, TILES * k + s + 1)
                act.activation(y_sb[:, :, TILE_ROWS * s:TILE_ROWS * (s + 1)],
                               ps_y[:, 0:TILE_ROWS * JPAD].rearrange("p (b j) -> p j b", j=JPAD),
                               ACT.Copy).then_inc(y_set, 1)

            def cin_features(k):
                act.wait_ge(l2_done, k + 1)
                act.activation(feat[:, 1, bass.ds(BLOCK_ROWS * k, BLOCK_ROWS)], y_sb[:, F, :],
                               ACT.Copy).then_inc(l1_feat_set, 1)
                act.activation(feat[:, 2, bass.ds(BLOCK_ROWS * k, BLOCK_ROWS)], ps_y[:, 0:BLOCK_ROWS],
                               ACT.Identity, bias=b2_d[:, 0:1]).then_inc(l2_feat_set, 1)

            def block_of(k, first, prepares):
                for p in range(SLOTS):
                    s, q = divmod(p, BANKS)
                    g = TILES * k + s
                    if q in ACT_BANKS:
                        n = ACT_BANKS.index(q)
                        if n == 0 and (s >= 2 or not first):
                            act.wait_ge(gp_steps, GP_STEPS * (g - 1))
                        act.wait_ge(bank_done, BANKS * g + q + 1)
                        for x in range(JB):
                            j = JB * q + x
                            ins = act.activation(prod[:, s % 2, n, H * x:H * (x + 1)],
                                                 ps_t[(BANKS * s + q) % T_RING][:, H * x:H * (x + 1)],
                                                 ACT.Copy, scale=x0_t[:, s, j:j + 1])
                        ins.then_inc(act_scaled, 1)
                    if p == position(0, 9) and not first:
                        store_y(k - 1, TILES - 1)
                    if p == position(2, 4) and not first:
                        cin_features(k - 1)
                    if p == position(2, 8):
                        if not first:
                            act.wait_ge(l1_feat_set, k)
                        store_y(k, 0)
                    if p == position(3, 1):
                        store_y(k, 1)
                    if q == 9 and s >= 3:
                        store_y(k, s - 1)
                    ahead, c, u = layer0_at(p)
                    if ahead == 0 or prepares:
                        layer0(k + ahead, c, u)
                    if prepares and p - 2 in TURN_AT:
                        turned(k + 1, TURN_AT.index(p - 2))

            act.wait_ge(w0_in, 16 * 3)
            act.activation(sel[:, :, :].rearrange("p t m -> p (t m)"), sel_raw, ACT.Copy).then_inc(sel_cast, 1)
            act.wait_ge(w0_folded, 1)
            act.activation(w0_hi[:, :, :].rearrange("p t h -> p (t h)"), w0_fwd_raw, ACT.Copy).then_inc(w0_split, 1)
            act.wait_ge(consts_in, 16 * 4)
            act.activation(b0_d[:, :], b0_sb[:, :], ACT.Copy, scale=float(D)).then_inc(bias_scaled, 1)
            act.activation(b2_d[:, :], b2_sb[:, :], ACT.Copy, scale=float(D)).then_inc(bias_scaled, 1)
            act.wait_ge(w1_in, 16)
            act.activation(w1_hi[:, :], w1_raw, ACT.Copy).then_inc(w1_hi_set, 1)
            act.wait_ge(bias_scaled, 2)
            act.wait_ge(zeroed, 1)
            for r in range(ETR):
                turned(0, r)
            for u in range(CHUNK_SLOTS):
                layer0(0, 0, u)
            act.wait_ge(w1_split, 1)
            act.wait_ge(w0_split, 2)
            block_of(0, True, True)
            with act.Fori(1, BLOCKS - 1) as k:
                block_of(k, False, True)
            block_of(BLOCKS - 1, False, False)
            store_y(BLOCKS - 1, TILES - 1)
            cin_features(BLOCKS - 1)
            for half in range(2):
                for m in range(TOP1 // P):
                    act.wait_ge(top_mm, 7 * half + m + 1)
                    if m == 0 and half == 1:
                        act.wait_ge(top_mm, 6)
                    act.activation(h1[:, m, :], ps_t[m][:, :], ACT.Relu, bias=bt1[:, m:m + 1]).then_inc(top_act, 1)
                for m in range(TOP2 // P):
                    act.wait_ge(top_mm, 7 * half + 5 + m)
                    act.activation(h2[:, m, :], (ps_sel[0], ps_x1)[m][:, :], ACT.Relu,
                                   bias=bt2[:, m:m + 1]).then_inc(top_act, 1)
                act.wait_ge(top_mm, 7 * half + 7)
                act.activation(y_out[:, 512 * half:512 * half + 512], ps_y[0:1, :], ACT.Copy).then_inc(top_act, 1)

        @block.vector
        def _(dve):
            def turned(k, r):
                ps = ps_sel[r % 2]
                dve.wait_ge(x0_hi_set, ETR * k + r + 1)
                dve.tensor_tensor(
                    x0[LO:SPLIT, :].rearrange("p (b d) -> p d b", d=D)[:, 4 * r:4 * r + 4, :],
                    ps[0:F, :].rearrange("p (d b) -> p d b", d=4),
                    x0[0:F, :].bitcast(F32).rearrange("p (b d) -> p d b", d=D)[:, 4 * r:4 * r + 4, :],
                    ALU.subtract).then_inc(x0_lo_set, 1)

            def layer0(k, c, u):
                chunk = CHUNKS * k + c
                cols = slice(c * CHUNK, (c + 1) * CHUNK)
                known = isinstance(chunk, int)
                t, r = divmod(u - Z_AT, STEP)
                if r == 0 and 0 <= t < UNITS:
                    n = UNITS * chunk + t
                    b = (c * UNITS + t) % Z_RING
                    if t == 0:
                        dve.wait_ge(copies_set, chunk + 1)
                    dve.wait_ge(shift_selected, n + 1)
                    if not (known and n < Z_RING):
                        was, tw = ring_before(chunk, t)
                        dve.wait_ge(z_lo_set(tw), low_part_count(was, tw))
                    dve.tensor_tensor(z[:, b, :], ps_sel[(t + 1) % 2][0:PAIRS, :], x0_copies[:, :],
                                      ALU.mult).then_inc(z_set, 1)
                t, r = divmod(u - Z_LO_AT, STEP)
                if r == 0 and t in DVE_LOW:
                    n = UNITS * chunk + t
                    b = (c * UNITS + t) % Z_RING
                    dve.wait_ge(z_hi_set, n + 1)
                    if not (known and n < Z_RING):
                        dve.wait_ge(z_used, n - Z_RING + 1)
                    dve.tensor_tensor(z_lo[:, b, :], z[:, b, :], z_hi[:, b, :].bitcast(F32),
                                      ALU.subtract).then_inc(z_lo_dve, 1)
                if u == X1_LO_AT:
                    dve.wait_ge(x1_hi_set, chunk + 1)
                    dve.scalar_tensor_tensor(x1_lo[:, cols], ps_x1[:, :], b0_sb[:, 0:1], x1_hi[:, cols].bitcast(F32),
                                             ALU.add, ALU.subtract).then_inc(x1_done, 1)
                    dve.tensor_reduce(feat[:, 0, bass.ds(BLOCK_ROWS * k + CHUNK // D * c, CHUNK // D)],
                                      ps_x1[:, :].rearrange("p (b d) -> p b d", d=D), AX.X,
                                      ALU.add).then_inc(x1_done, 1)

            def join(k, s, step, early):
                g = TILES * k + s
                mine = dve_sum[:, s % 2].rearrange("p a h -> p (a h)")
                if step == 0:
                    dve.wait_ge(gp_steps, GP_STEPS * (g + 1))
                    dve.wait_ge(dve_steps, DVE_UNITS * (g + 1))
                    dve.tensor_tensor(mine, mine, gp_sum[:, s % 2].rearrange("p a h -> p (a h)"),
                                      ALU.add).then_inc(joined, 1)
                else:
                    dve.wait_ge(joined, 2 * g + 1)
                    if not early:
                        dve.wait_ge(y_done, g - 3)
                    dve.tensor_tensor(x2[:, s % 4, :], dve_sum[:, s % 2, 0, :], dve_sum[:, s % 2, 1, :],
                                      ALU.add).then_inc(joined, 1)

            def block_of(k, first, prepares):
                for p in range(SLOTS):
                    s, q = divmod(p, BANKS)
                    g = TILES * k + s
                    if q in DVE_BANKS:
                        if q == DVE_BANKS[0] and s % TPC == 0:
                            dve.wait_ge(x0_t_set, CHUNKS * k + s // TPC + 1)
                        for x in range(FIELDS_OF[q]):
                            n = dve_units_before(q) + x
                            j = JB * q + x
                            mine = dve_sum[:, s % 2, n % 2, :]
                            t_j = ps_t[(BANKS * s + q) % T_RING][:, H * x:H * (x + 1)]
                            if n >= 2:
                                dve.wait_ge(dve_steps, DVE_UNITS * g + n - 1)
                            elif n == 0 and (s >= 2 or not first):
                                dve.wait_ge(joined, 2 * (g - 1))
                            if x == 0:
                                dve.wait_ge(bank_done, BANKS * g + q + 1)
                            if n == 1:
                                dve.tensor_scalar(mine, t_j, x0_t[:, s, j:j + 1], None, ALU.mult).then_inc(dve_steps, 1)
                            else:
                                dve.scalar_tensor_tensor(mine, t_j, x0_t[:, s, j:j + 1], b1_sb[:, :] if n == 0 else mine,
                                                         ALU.mult, ALU.add).then_inc(dve_steps, 1)
                    if q in JOIN_AT and s > 0:
                        join(k, s - 1, JOIN_AT.index(q), first and s - 1 < 4)
                    if q in JOIN_AT and s == 0 and not first:
                        join(k - 1, TILES - 1, JOIN_AT.index(q), False)
                    ahead, c, u = layer0_at(p)
                    if ahead == 0 or prepares:
                        layer0(k + ahead, c, u)
                    if prepares and p - 3 in TURN_AT:
                        turned(k + 1, TURN_AT.index(p - 3))

            dve.wait_ge(w0_in, 16 * 3)
            dve.tensor_tensor(w0_fwd_raw, w0_fwd_raw, w0_rev_raw, ALU.add).then_inc(w0_folded, 1)
            dve.wait_ge(w0_split, 1)
            dve.tensor_tensor(w0_lo[:, :, :].rearrange("p t h -> p (t h)"), w0_fwd_raw,
                              w0_hi[:, :, :].rearrange("p t h -> p (t h)").bitcast(F32),
                              ALU.subtract).then_inc(w0_split, 1)
            dve.wait_ge(w1_hi_set, 1)
            dve.tensor_tensor(w1_lo[:, :], w1_raw, w1_hi[:, :].bitcast(F32), ALU.subtract).then_inc(w1_split, 1)
            dve.wait_ge(consts_in, 16 * 4)
            for r in range(ETR):
                turned(0, r)
            for u in range(CHUNK_SLOTS):
                layer0(0, 0, u)
            block_of(0, True, True)
            with dve.Fori(1, BLOCKS - 1) as k:
                block_of(k, False, True)
            block_of(BLOCKS - 1, False, False)
            join(BLOCKS - 1, TILES - 1, 0, False)
            join(BLOCKS - 1, TILES - 1, 1, False)
            dve.wait_ge(x1_done, 2 * CHUNKS * BLOCKS)
            dve.wait_ge(bias_scaled, 2)
            dve.tensor_scalar(feat[:, 0, :], feat[:, 0, :], b0_d[:, 0:1], None, ALU.add).then_inc(feat0_done, 1)

        @block.tensor
        def _(pe):
            def turn(k, r):
                ps = ps_sel[r % 2]
                known = isinstance(k, int)
                if r == 0:
                    pe.wait_ge(emb_in, 16 * F * (k + 1))
                if r < 2 and not (known and k == 0):
                    pe.wait_ge(z_set, UNITS * CHUNKS * k - 1 + r)
                if r >= 2:
                    pe.wait_ge(x0_lo_set, ETR * k + r - 1)
                pe.nop(nofuse=True)
                for x in range(4):
                    ins = pe.transpose(ps[0:F, BLOCK_ROWS * x:BLOCK_ROWS * (x + 1)],
                                       emb[:, :].rearrange("p (j d) -> p d j", d=D)[:, 4 * r + x, :],
                                       ident_sb[:, :])
                ins.then_inc(emb_turned, 1)

            def layer0(k, c, u):
                chunk = CHUNKS * k + c
                known = isinstance(chunk, int)
                cols = slice(c * CHUNK, (c + 1) * CHUNK)
                if u == 0:
                    pe.wait_ge(x0_lo_set, ETR * (k + 1))
                    if not (known and chunk == 0):
                        pe.wait_ge(z_set, UNITS * chunk - 1)
                    pe.matmul(ps_sel[0][0:PAIRS, :], sel[:, UNITS, :], x0[:, cols], start=True,
                              stop=True).then_inc(copies_selected, 1)
                if u == X0_TURN_AT:
                    pe.wait_ge(copies_set, chunk + 1)
                    if not (known and chunk == 0):
                        pe.wait_ge(x1_done, 2 * chunk)
                    for t in range(TPC):
                        ins = pe.transpose(ps_x1[:, P * t:P * t + PAIRS], x0_copies[:, P * t:P * (t + 1)],
                                           ident_sb[0:PAIRS, 0:PAIRS])
                    ins.then_inc(x0_turned, 1)
                t, r = divmod(u - SELECT_AT, STEP)
                if r == 0 and 0 <= t < UNITS:
                    n = UNITS * chunk + t
                    if t == 1:
                        pe.wait_ge(copies_set, chunk + 1)
                    elif not (known and n == 0):
                        pe.wait_ge(z_set, n - (t > 0))
                    pe.matmul(ps_sel[(t + 1) % 2][0:PAIRS, :], sel[:, t, :], x0[:, cols], start=True,
                              stop=True).then_inc(shift_selected, 1)
                t, r = divmod(u - SUM_AT, STEP)
                if r == 0 and 0 <= t < UNITS:
                    n = UNITS * chunk + t
                    b = (c * UNITS + t) % Z_RING
                    if t == 0:
                        pe.wait_ge(x0_t_set, chunk + 1)
                    pe.wait_ge(z_lo_set(t), low_part_count(chunk, t))
                    pe.matmul(ps_x1[:, :], w0_hi[:, t, :], z_hi[:, b, :], start=(t == 0), stop=False)
                    pe.matmul(ps_x1[:, :], w0_lo[:, t, :], z_hi[:, b, :], start=False, stop=False)
                    pe.matmul(ps_x1[:, :], w0_hi[:, t, :], z_lo[:, b, :], start=False,
                              stop=(t == UNITS - 1)).then_inc(z_used, 1)

            def sum_over_d(k, s):
                g = TILES * k + s
                c = s // TPC
                if s % TPC == 0:
                    pe.wait_ge(diag_in[c % 2], 16 * TILE_ROWS * (2 * k + c // 2 + 1))
                if s > 0:
                    pe.wait_ge(y_set, g)
                elif not (isinstance(k, int) and k == 0):
                    pe.wait_ge(l2_feat_set, k)
                pe.wait_ge(joined, 2 * (g + 1))
                pe.matmul(ps_y[:, 0:TILE_ROWS * JPAD], x2[:, s % 4, :],
                          x0_diag[:, s % DIAG_RING].rearrange("p b j -> p (b j)"), start=True, stop=True).then_inc(y_done, 1)

            def layer2(k, j):
                if j == 0:
                    pe.wait_ge(y_set, TILES * (k + 1))
                ins = pe.matmul(ps_y[:, 0:BLOCK_ROWS], w2_sb[:, j, :], y_sb[:, j, :], start=(j == 0), stop=(j == F - 1))
                if j == F - 1:
                    ins.then_inc(l2_done, 1)

            def block_of(k, first, prepares):
                for p in range(SLOTS):
                    s, q = divmod(p, BANKS)
                    g = TILES * k + s
                    if q == 0 and s % TPC == 0:
                        pe.wait_ge(x1_done, 2 * (CHUNKS * k + s // TPC) + 1)
                    if not (first and p < T_RING):
                        so, qo = divmod(p - T_RING, BANKS)
                        go = TILES * k + so
                        if qo in ACT_BANKS:
                            pe.wait_ge(act_scaled, len(ACT_BANKS) * go + act_banks_before(qo) + 1)
                        else:
                            pe.wait_ge(dve_steps, DVE_UNITS * go + dve_units_before(qo + 1))
                    w = FIELDS_OF[q] * H
                    ps = ps_t[p % T_RING][:, 0:w]
                    cols = slice(P * s, P * (s + 1))
                    js = slice(JB * H * q, JB * H * q + w)
                    pe.matmul(ps, x1_hi[:, cols], w1_hi[:, js], start=True, stop=False)
                    pe.matmul(ps, x1_hi[:, cols], w1_lo[:, js], start=False, stop=False)
                    pe.matmul(ps, x1_lo[:, cols], w1_hi[:, js], start=False, stop=True).then_inc(bank_done, 1)
                    if p == position(0, 8) and not first:
                        sum_over_d(k - 1, TILES - 1)
                    if not first and L2_FROM <= p < L2_FROM + L2_SLOTS:
                        for j in range(L2_EACH * (p - L2_FROM), min(F, L2_EACH * (p - L2_FROM + 1))):
                            layer2(k - 1, j)
                    if p == position(2, 7):
                        sum_over_d(k, 0)
                    if p == position(3, 0):
                        sum_over_d(k, 1)
                    if q == 8 and s >= 3:
                        sum_over_d(k, s - 1)
                    ahead, c, u = layer0_at(p)
                    if ahead == 0 or prepares:
                        layer0(k + ahead, c, u)
                    if prepares and p in TURN_AT:
                        turn(k + 1, TURN_AT.index(p))

            pe.wait_ge(consts_in, 16 * 4)
            for r in range(ETR):
                turn(0, r)
            pe.wait_ge(sel_cast, 1)
            pe.wait_ge(w0_split, 2)
            for u in range(CHUNK_SLOTS):
                layer0(0, 0, u)
            pe.wait_ge(w1_split, 1)
            block_of(0, True, True)
            pe.wait_ge(w2_in, 16)
            with pe.Fori(1, BLOCKS - 1) as k:
                block_of(k, False, True)
            block_of(BLOCKS - 1, False, False)
            sum_over_d(BLOCKS - 1, TILES - 1)
            for j in range(F):
                layer2(BLOCKS - 1, j)
            pe.wait_ge(top_in, 16 * 7)
            pe.wait_ge(feat0_done, 1)
            pe.wait_ge(l2_feat_set, BLOCKS)
            for half in range(2):
                rows = slice(512 * half, 512 * half + 512)
                for m in range(TOP1 // P):
                    if half == 0:
                        pe.wait_ge(dve_steps, DVE_UNITS * TILES * BLOCKS)
                        pe.wait_ge(act_scaled, len(ACT_BANKS) * TILES * BLOCKS)
                    else:
                        pe.wait_ge(top_act, m + 1)
                    for n in range(N_CIN):
                        pe.matmul(ps_t[m][:, :], wt1[:, n, P * m:P * (m + 1)], feat[:, n, rows], start=(n == 0), stop=False)
                    pe.matmul(ps_t[m][:, :], wt1_dense[:, P * m:P * (m + 1)], dense[:, rows], start=False,
                              stop=True).then_inc(top_mm, 1)
                for m in range(TOP2 // P):
                    pe.wait_ge(top_act, 7 * half + TOP1 // P)
                    for n in range(TOP1 // P):
                        ins = pe.matmul((ps_sel[0], ps_x1)[m][:, :], wt2[:, n, P * m:P * (m + 1)], h1[:, n, :],
                                        start=(n == 0), stop=(n == TOP1 // P - 1))
                    ins.then_inc(top_mm, 1)
                pe.wait_ge(top_act, 7 * half + 6)
                for n in range(TOP2 // P):
                    ins = pe.matmul(ps_y[0:1, :], wt3[:, n:n + 1], h2[:, n, :], start=(n == 0), stop=(n == TOP2 // P - 1))
                ins.then_inc(top_mm, 1)


def _pair_layout(w, reverse):
    import numpy as np
    o = np.zeros((COPIES, F, UNITS, H), w.dtype)
    j = np.arange(F)
    for t in range(UNITS):
        for g in range(COPIES):
            s = COPIES * t + g
            if s > F // 2 or (reverse and s == 0):
                continue
            k = (j + s) % F
            o[g, :, t, :] = (w[:, k, j] if reverse else w[:, j, k]).T
    return o.reshape(PAIRS, UNITS * H)


def _select_layout():
    import numpy as np
    o = np.zeros((SPLIT, UNITS + 1, COPIES, F), np.float32)
    for t in range(UNITS + 1):
        for g in range(COPIES):
            s = 0 if t == UNITS else COPIES * t + g
            for j in range(F):
                o[(j + s) % F, t, g, j] = 1.0
                o[LO + (j + s) % F, t, g, j] = 1.0
    return o.reshape(SPLIT, (UNITS + 1) * PAIRS)


def kernel(**inputs):
    import numpy as np
    import concourse.bacc as _bacc
    from concourse import mybir as _mybir
    from concourse.bass_utils import run_bass_kernel_spmd as _run

    a = {n: np.asarray(v) for n, v in inputs.items()}
    mask = np.zeros((P, TILE_ROWS, JPAD), np.float32)
    for p in range(P):
        mask[p, p // D, F] = 1.0
    arrays = {
        "ids": a["ids"].reshape(BLOCKS, BLOCK_ROWS, F),
        "dense_t": a["dense_ctx"].T,
        "w0_fwd": _pair_layout(a["L0_rec_W0"].reshape(H, F, F), False),
        "w0_rev": _pair_layout(a["L0_rec_W0"].reshape(H, F, F), True),
        "w1": a["L0_rec_W1"].reshape(H, F, H).transpose(2, 1, 0).reshape(H, F * H),
        "w2": a["L0_rec_W2"].reshape(H, F, H).transpose(2, 1, 0),
        "b0": a["L0_rec_b0"].reshape(H, 1),
        "b1_rows": np.broadcast_to(a["L0_rec_b1"], (P, H)),
        "b2": a["L0_rec_b2"].reshape(H, 1),
        "select": _select_layout(),
        "ident": np.eye(P, dtype=np.float32),
        "mask": mask,
        "w_top1": a["W_top1"][:N_CIN * H].reshape(N_CIN, H, TOP1).transpose(1, 0, 2),
        "w_top1_dense": a["W_top1"][N_CIN * H:],
        "b_top1": a["b_top1"].reshape(TOP1 // P, P).T,
        "w_top2": a["W_top2"].reshape(TOP1 // P, P, TOP2).transpose(1, 0, 2),
        "b_top2": a["b_top2"].reshape(TOP2 // P, P).T,
        "w_top3": a["W_top3"].reshape(TOP2 // P, P).T,
    }
    for f in range(F):
        arrays[f"tbl_{f}"] = a[f"tbl_{f}"]
    nc = _bacc.Bacc("TRN2", target_bir_lowering=False, num_devices=1)
    args, maps = {}, {}
    for n, v in arrays.items():
        v = np.ascontiguousarray(v)
        maps[f"in_{n}"] = v
        args[n] = nc.dram_tensor(f"in_{n}", v.shape, _mybir.dt.from_np(v.dtype), kind="ExternalInput").ap()
    tables = [args.pop(f"tbl_{f}") for f in range(F)]
    out = nc.dram_tensor("out_0", (B, 1), _mybir.dt.float32, kind="ExternalOutput").ap()
    cin_tower(nc, **args, out=out, tables=tables)
    return _run(nc, [maps], core_ids=[0]).results[0]["out_0"]
```

```python
from contextlib import ExitStack

import concourse.bass as bass
from concourse import mybir

F32 = mybir.dt.float32
F32R = mybir.dt.float32r
I32 = mybir.dt.int32
ALU = mybir.AluOpType
ACT = mybir.ActivationFunctionType
AX = mybir.AxisListType

P = 128
B, F, D, H = 1024, 39, 16, 128
N_CIN = 3
DENSE = 16
HALF = B // 2
TOP1, TOP2 = 512, 256
BLOCK_ROWS = 128
BLOCKS = B // BLOCK_ROWS
BLOCK_COLS = BLOCK_ROWS * D
CHUNKS = 4
CHUNK = BLOCK_COLS // CHUNKS
TILES = BLOCK_COLS // P
TPC = TILES // CHUNKS
TILE_ROWS = P // D
COPIES = 3
PAIRS = COPIES * F
UNITS = -(-(F // 2 + 1) // COPIES)
JB = 4
BANKS = -(-F // JB)
JPAD = F + 1

T_RING = 5
Z_RING = 4
A_RING = 4
DIAG_RING = 2 * TPC

ACT_BANKS = (0, 2, 4, 6, 8)
FIELDS_OF = [min(JB, F - JB * q) for q in range(BANKS)]
DVE_BANKS = tuple(q for q in range(BANKS) if q not in ACT_BANKS)
DVE_UNITS = sum(FIELDS_OF[q] for q in DVE_BANKS)
DVE_ADDS = 4
GP_ADDS = {1: 3, 2: 5, 3: 7}
GP_STEPS = len(GP_ADDS) + 1
DVE_LOW = tuple(range(1, UNITS, 2))

SLOTS = TILES * BANKS
CHUNK_SLOTS = TPC * BANKS
JOIN_AT = (1, 3, 5, 7)
JOINS = len(JOIN_AT)
STEP = 5
Z_AT, Z_HI_AT, Z_LO_AT, SUM_AT = -8, -5, -4, 4
X0_TURN_AT, X0_T_AT, X1_HI_AT, X1_LO_AT = 1, 3, 35, 36
Y_AT = [42, 46, 50, 55] + [BANKS * (s + 2) + 4 for s in range(4, TILES)]
L2_FROM, L2_SLOTS, L2_EACH = 19, 20, 2
ETR = 4
TURN_AT = [2 * CHUNK_SLOTS + x for x in (7, 11, 15, 19)]
GATHER_FROM, GATHER_STEP = 3 * CHUNK_SLOTS - 8, 3
GATHERS_FIRST = -(-(SLOTS - GATHER_FROM) // GATHER_STEP)
GATHERS_IDLE, GATHERS_START = 6, 11
TOP_STEPS = 2 * (TOP1 // P + TOP2 // P + 1)


def dve_units_before(q):
    return sum(FIELDS_OF[x] for x in DVE_BANKS if x < q)


def low_part_count(chunk, t):
    return (UNITS // 2 if t in DVE_LOW else UNITS - UNITS // 2) * chunk + t // 2 + 1


def cin_tower(nc, ids, dense_t, w0_fwd, w0_rev, w1, w2, b0, b1_rows, b2, ident, mask,
              w_top1, w_top1_dense, b_top1, w_top2, b_top2, w_top3, out, tables):
    with ExitStack() as ctx:
        def sb(name, shape, dt=F32):
            return ctx.enter_context(nc.sbuf_tensor(name, shape, dt))

        def bank(name):
            return ctx.enter_context(nc.psum_tensor(name, [P, 512], F32))

        def sem(name):
            return ctx.enter_context(nc.semaphore(name))

        w1_hi = sb("w1_hi", [P, F * H], F32R)
        w1_lo = sb("w1_lo", [P, F * H], F32R)
        w2_sb = sb("w2_sb", [P, F, H])
        w0_hi = sb("w0_hi", [PAIRS, UNITS, H], F32R)
        w0_lo = sb("w0_lo", [PAIRS, UNITS, H], F32R)
        ident_sb = sb("ident_sb", [P, P])
        b0_sb = sb("b0_sb", [P, 1])
        b1_sb = sb("b1_sb", [P, H])
        b2_sb = sb("b2_sb", [P, 1])
        b0_d = sb("b0_d", [P, 1])
        b2_d = sb("b2_d", [P, 1])
        wt1 = sb("wt1", [P, N_CIN, TOP1])
        wt1_dense = sb("wt1_dense", [DENSE, TOP1])
        wt3 = sb("wt3", [P, TOP2 // P])
        bt1 = sb("bt1", [P, TOP1 // P])
        bt2 = sb("bt2", [P, TOP2 // P])
        ids_cur = sb("ids_cur", [P, F], I32)
        emb = sb("emb", [P, F * D])
        x0 = sb("x0", [2 * F, BLOCK_COLS])
        x0_copies = sb("x0_copies", [PAIRS, 2, CHUNK])
        x0_shifted = sb("x0_shifted", [PAIRS, A_RING, CHUNK])
        x0_t = sb("x0_t", [P, TILES, JPAD])
        z = sb("z", [PAIRS, Z_RING, CHUNK])
        z_hi = sb("z_hi", [PAIRS, Z_RING, CHUNK], F32R)
        z_lo = sb("z_lo", [PAIRS, Z_RING, CHUNK], F32R)
        x1_hi = sb("x1_hi", [P, BLOCK_COLS], F32R)
        x1_lo = sb("x1_lo", [P, BLOCK_COLS], F32R)
        prod = sb("prod", [P, 2, len(ACT_BANKS), JB * H])
        gp_sum = sb("gp_sum", [P, 2, 2, H])
        dve_sum = sb("dve_sum", [P, 2, 2, H])
        x2 = sb("x2", [P, 4, H])
        x0_diag = sb("x0_diag", [P, DIAG_RING, TILE_ROWS, JPAD])
        y_sb = sb("y_sb", [P, JPAD, BLOCK_ROWS])
        feat = sb("feat", [P, N_CIN, B])
        dense = x0_shifted[0:DENSE, 0:B // CHUNK, :].rearrange("p a n -> p (a n)")
        wt2 = x0_diag[:, 0:TPC].rearrange("p a b j -> p (a b j)")[:, 0:TOP1 // P * TOP2].rearrange(
            "p (n m) -> p n m", n=TOP1 // P)
        w2_flat = w2_sb[:, :, :].rearrange("p j h -> p (j h)")
        h1 = [prod[:, 0, 0:TOP1 // P, :], w2_flat[:, 0:TOP1 // P * HALF].rearrange("p (m n) -> p m n", n=HALF)]
        h2 = [w2_flat[:, x * HALF:(x + TOP2 // P) * HALF].rearrange("p (m n) -> p m n", n=HALF) for x in (4, 6)]
        y_out = y_sb[0:1, 0:B // BLOCK_ROWS, :].rearrange("p j b -> p (j b)")
        w1_raw = y_sb[:, 0:F, :].rearrange("p j h -> p (j h)")
        raw = prod[:, :, :, :].rearrange("p a b c -> p (a b c)")
        n_w0 = UNITS * H
        w0_fwd_raw = raw[0:PAIRS, 0:n_w0]
        w0_rev_raw = raw[0:PAIRS, n_w0:2 * n_w0]

        ps_t = [bank(f"ps_t{i}") for i in range(T_RING)]
        ps_turn = bank("ps_turn")
        ps_x1 = bank("ps_x1")
        ps_y = bank("ps_y")

        consts_in = sem("consts_in")
        mask_in = sem("mask_in")
        w0_in = sem("w0_in")
        w1_in = sem("w1_in")
        w2_in = sem("w2_in")
        top_in = sem("top_in")
        wt2_in = sem("wt2_in")
        ids_in = sem("ids_in")
        emb_in = sem("emb_in")
        out_done = sem("out_done")
        w0_folded = sem("w0_folded")
        w0_split = sem("w0_split")
        w1_hi_set = sem("w1_hi_set")
        w1_split = sem("w1_split")
        bias_scaled = sem("bias_scaled")
        emb_turned = sem("emb_turned")
        x0_set = sem("x0_set")
        x0_twice = sem("x0_twice")
        copies_in = [sem(f"copies_in{i}") for i in range(2)]
        shifted_in = [sem(f"shifted_in{i}") for i in range(A_RING)]
        x0_turned = sem("x0_turned")
        x0_t_set = sem("x0_t_set")
        z_set = sem("z_set")
        z_hi_set = sem("z_hi_set")
        z_lo_gp = sem("z_lo_gp")
        z_lo_dve = sem("z_lo_dve")
        z_used = sem("z_used")
        x1_hi_set = sem("x1_hi_set")
        x1_done = sem("x1_done")
        bank_done = sem("bank_done")
        dve_steps = sem("dve_steps")
        act_scaled = sem("act_scaled")
        gp_steps = sem("gp_steps")
        joined = sem("joined")
        diag_in = [sem(f"diag_in{i}") for i in range(2)]
        y_done = sem("y_done")
        y_set = sem("y_set")
        l2_done = sem("l2_done")
        l1_feat_set = sem("l1_feat_set")
        l2_feat_set = sem("l2_feat_set")
        feat0_done = sem("feat0_done")
        top_mm = sem("top_mm")
        top_act = sem("top_act")

        top2_banks = ((ps_turn, ps_x1), (ps_t[4], ps_t[0]))
        top3_banks = (ps_t[1], ps_y)

        block = ctx.enter_context(nc.Block())

        def z_lo_set(t):
            return z_lo_dve if t in DVE_LOW else z_lo_gp

        def ring_before(chunk, t):
            return (chunk, t - Z_RING) if t >= Z_RING else (chunk - 1, t - Z_RING + UNITS)

        def turn_bank(k, r):
            return ps_t[r] if once(k) and k == 0 else ps_turn

        def layer0_at(p):
            c, u = p // CHUNK_SLOTS + 1, p % CHUNK_SLOTS
            return [(c // CHUNKS, c % CHUNKS, u), ((c + 1) // CHUNKS, (c + 1) % CHUNKS, u - CHUNK_SLOTS)]

        def once(count):
            return isinstance(count, int)

        def layer0_first():
            return [x for u in range(-CHUNK_SLOTS, CHUNK_SLOTS) for x in ((0, u), (1, u - CHUNK_SLOTS))]

        @block.sync
        def _(sp):
            sp.dma_start(ids_cur[:, :], ids[0]).then_inc(ids_in, 16)
            sp.dma_start(ident_sb[:, :], ident).then_inc(consts_in, 16)
            for i in range(DIAG_RING):
                sp.dma_start(x0_diag[:, i], mask).then_inc(mask_in, 16)
            sp.dma_start(b0_sb[:, :], b0).then_inc(consts_in, 16)
            sp.dma_start(b1_sb[:, :], b1_rows).then_inc(consts_in, 16)
            sp.dma_start(b2_sb[:, :], b2).then_inc(consts_in, 16)
            sp.dma_start(w0_fwd_raw, w0_fwd).then_inc(w0_in, 16)
            sp.dma_start(w0_rev_raw, w0_rev).then_inc(w0_in, 16)
            sp.dma_start(w1_raw, w1).then_inc(w1_in, 16)
            sp.dma_start(w2_sb[:, :, :], w2).then_inc(w2_in, 16)
            for t, d in ((wt1[:, :, :], w_top1), (wt1_dense[:, :], w_top1_dense), (bt1[:, :], b_top1),
                         (bt2[:, :], b_top2), (wt3[:, :], w_top3)):
                sp.dma_start(t, d).then_inc(top_in, 16)

            def next_ids(k):
                sp.wait_ge(emb_in, 16 * F * k)
                src = ids[k] if once(k) else ids[bass.ds(k, 1)].rearrange("a p f -> (a p) f")
                sp.dma_start(ids_cur[:, :], src).then_inc(ids_in, 16)

            def diagonal(k, c):
                chunk = CHUNKS * k + c
                sp.wait_ge(x0_t_set, chunk + 1)
                sp.nop(nofuse=True)
                if not (once(chunk) and chunk < 2):
                    sp.wait_ge(y_done, TPC * (chunk - 1))
                for r in range(TILE_ROWS):
                    rows = slice(D * r, D * r + D)
                    sp.dma_start(x0_diag[rows, TPC * (c % 2):TPC * (c % 2 + 1), r, 0:F],
                                 x0_t[rows, TPC * c:TPC * (c + 1), 0:F]).then_inc(diag_in[c % 2], 16)

            def shift(k, c, t):
                n = UNITS * (CHUNKS * k + c) + t
                place = (UNITS * c + t) % A_RING
                if not (once(n) and n < A_RING):
                    sp.wait_ge(z_set, n - A_RING + 1)
                for g in range(COPIES):
                    by = min(COPIES * t + g, F // 2)
                    sp.dma_start(x0_shifted[F * g:F * (g + 1), place, :],
                                 x0[by:by + F, CHUNK * c:CHUNK * (c + 1)]).then_inc(shifted_in[place], 16)

            def chunk_inputs(k, c):
                chunk = CHUNKS * k + c
                if c == 0:
                    sp.wait_ge(x0_set, ETR * (k + 1))
                    sp.dma_start(x0[F:2 * F, :], x0[0:F, :]).then_inc(x0_twice, 16)
                if not (once(chunk) and chunk < 2):
                    sp.wait_ge(x0_turned, chunk - 1)
                    sp.nop(nofuse=True)
                    sp.wait_ge(z_set, UNITS * (chunk - 1))
                for g in range(COPIES):
                    sp.dma_start(x0_copies[F * g:F * (g + 1), c % 2, :],
                                 x0[0:F, CHUNK * c:CHUNK * (c + 1)]).then_inc(copies_in[c % 2], 16)
                if c == 0:
                    sp.wait_ge(x0_twice, 16 * (k + 1))
                    sp.nop(nofuse=True)
                for t in range(UNITS):
                    shift(k, c, t)
                    if t == 2 and not (once(chunk) and chunk == 0):
                        diagonal(k if c > 0 else k - 1, (c - 1) % CHUNKS)

            next_ids(1)
            sp.wait_ge(mask_in, 16 * DIAG_RING)
            for c in range(CHUNKS):
                chunk_inputs(0, c)
            next_ids(2)
            chunk_inputs(1, 0)
            with sp.Fori(1, BLOCKS - 2) as k:
                for c in range(1, CHUNKS):
                    chunk_inputs(k, c)
                next_ids(k + 2)
                chunk_inputs(k + 1, 0)
            for c in range(1, CHUNKS):
                chunk_inputs(BLOCKS - 2, c)
            for c in range(CHUNKS):
                chunk_inputs(BLOCKS - 1, c)
            diagonal(BLOCKS - 1, CHUNKS - 1)
            sp.wait_ge(z_set, UNITS * CHUNKS * BLOCKS)
            sp.dma_start(dense, dense_t).then_inc(top_in, 16)
            sp.wait_ge(y_done, TILES * BLOCKS - TPC)
            sp.dma_start(wt2, w_top2).then_inc(wt2_in, 16)
            sp.wait_ge(top_act, TOP_STEPS)
            sp.dma_start(out.rearrange("b a -> a b"), y_out[:, :]).then_inc(out_done, 16)
            sp.wait_ge(out_done, 16)

        @block.gpsimd
        def _(gp):
            def gather(f):
                gp.indirect_dma_start(emb[:, D * f:D * f + D], None, tables[f],
                                      bass.IndirectOffsetOnAxis(ap=ids_cur[:, f:f + 1], axis=0)).then_inc(emb_in, 16)

            def layer0(k, c, u):
                t, r = divmod(u - Z_LO_AT, STEP)
                if r == 0 and 0 <= t < UNITS and t not in DVE_LOW:
                    n = (k * CHUNKS + c) * UNITS + t
                    b = (c * UNITS + t) % Z_RING
                    gp.wait_ge(z_hi_set, n + 1)
                    if not (once(n) and n < Z_RING):
                        gp.wait_ge(z_used, n - Z_RING + 1)
                    gp.tensor_tensor(z_lo[:, b, :], z[:, b, :], z_hi[:, b, :].bitcast(F32),
                                     ALU.subtract).then_inc(z_lo_gp, 1)

            def add(k, s, n, early):
                g = TILES * k + s
                pair = prod[:, s % 2]
                x = list(GP_ADDS).index(n)
                if x > 0:
                    gp.wait_ge(gp_steps, GP_STEPS * g + x)
                gp.wait_ge(act_scaled, len(ACT_BANKS) * g + n + 1)
                gp.tensor_tensor(pair[:, 0, :], pair[:, 0, :], pair[:, n, :], ALU.add).then_inc(gp_steps, 1)
                if x == len(GP_ADDS) - 1:
                    gp.wait_ge(gp_steps, GP_STEPS * g + x + 1)
                    if not (early and s < 2):
                        gp.wait_ge(joined, JOINS * (g - 1))
                    gp.tensor_tensor(gp_sum[:, s % 2].rearrange("p a h -> p (a h)"), pair[:, 0, 0:2 * H],
                                     pair[:, 0, 2 * H:4 * H], ALU.add).then_inc(gp_steps, 1)

            def block_of(k, gathered, first, prepares, gathers):
                for p in range(SLOTS):
                    s, q = divmod(p, BANKS)
                    for n, at in GP_ADDS.items():
                        if q == at % BANKS and not (first and p < at):
                            add(k, s - at // BANKS, n, first)
                    for ahead, c, u in layer0_at(p):
                        if ahead == 0 or prepares:
                            layer0(k + ahead, c, u)
                    f, r = divmod(p - GATHER_FROM, GATHER_STEP)
                    if gathers and r == 0 and f >= 0:
                        if f == 0:
                            gp.wait_ge(emb_turned, ETR * (k + 2))
                            gp.wait_ge(ids_in, 16 * (k + 3))
                            gp.nop(nofuse=True)
                        gather(f)
                    f, r = divmod(p, GATHER_STEP)
                    if prepares and r == 0 and f + gathered < F:
                        if f == 0:
                            gp.nop(nofuse=True)
                        gather(f + gathered)

            gp.wait_ge(ids_in, 16)
            for f in range(F):
                gather(f)
            gp.wait_ge(emb_turned, ETR)
            gp.wait_ge(ids_in, 16 * 2)
            for f in range(GATHERS_IDLE):
                gather(f)
            f = GATHERS_IDLE
            for c, u in layer0_first():
                layer0(0, c, u)
                if c == 0 and (u - Z_LO_AT) % STEP == 0 and Z_LO_AT < u and f < GATHERS_START:
                    gather(f)
                    f += 1
            block_of(0, GATHERS_START, True, True, True)
            with gp.Fori(1, BLOCKS - 2) as k:
                block_of(k, GATHERS_FIRST, False, True, True)
            block_of(BLOCKS - 2, GATHERS_FIRST, False, True, False)
            block_of(BLOCKS - 1, 0, False, False, False)
            for n, at in GP_ADDS.items():
                if at >= BANKS:
                    add(BLOCKS - 1, TILES - 1, n, False)

        @block.scalar
        def _(act):
            def turned(k, r):
                if r == 0 and not (once(k) and k == 0):
                    act.wait_ge(copies_in[1], 16 * COPIES * (CHUNKS // 2) * k)
                    for place in range(A_RING):
                        act.wait_ge(shifted_in[place], 16 * COPIES * (UNITS * CHUNKS // A_RING) * k)
                act.wait_ge(emb_turned, ETR * k + r + 1)
                act.activation(
                    x0[0:F, :].rearrange("p (b d) -> p d b", d=D)[:, 4 * r:4 * r + 4, :],
                    turn_bank(k, r)[0:F, :].rearrange("p (d b) -> p d b", d=4), ACT.Copy).then_inc(x0_set, 1)

            def layer0(k, c, u):
                chunk = CHUNKS * k + c
                cols = slice(c * CHUNK, (c + 1) * CHUNK)
                known = once(chunk)
                if u == X0_T_AT:
                    act.wait_ge(x0_turned, chunk + 1)
                    if not (known and chunk < CHUNKS):
                        act.wait_ge(dve_steps, DVE_UNITS * TPC * (chunk - CHUNKS + 1))
                        act.wait_ge(diag_in[c % 2], 16 * TILE_ROWS * (2 * k + c // 2 - 1))
                    act.activation(
                        x0_t[:, TPC * c:TPC * (c + 1), 0:F],
                        ps_turn[:, :].rearrange("p (t j) -> p t j", t=TPC)[:, :, 0:F],
                        ACT.Copy).then_inc(x0_t_set, 1)
                t, r = divmod(u - Z_HI_AT, STEP)
                if r == 0 and 0 <= t < UNITS:
                    n = UNITS * chunk + t
                    b = (c * UNITS + t) % Z_RING
                    act.wait_ge(z_set, n + 1)
                    if not (known and n < Z_RING):
                        act.wait_ge(z_used, n - Z_RING + 1)
                        was, tw = ring_before(chunk, t)
                        act.wait_ge(z_lo_set(tw), low_part_count(was, tw))
                    act.activation(z_hi[:, b, :], z[:, b, :], ACT.Copy).then_inc(z_hi_set, 1)
                if u == X1_HI_AT:
                    act.wait_ge(z_used, UNITS * (chunk + 1))
                    if not (known and chunk < CHUNKS):
                        act.wait_ge(bank_done, BANKS * TPC * (chunk - CHUNKS + 1))
                    act.activation(x1_hi[:, cols], ps_x1[:, :], ACT.Identity,
                                   bias=b0_sb[:, 0:1]).then_inc(x1_hi_set, 1)

            def store_y(k, s):
                act.wait_ge(y_done, TILES * k + s + 1)
                act.activation(y_sb[:, :, TILE_ROWS * s:TILE_ROWS * (s + 1)],
                               ps_y[:, 0:TILE_ROWS * JPAD].rearrange("p (b j) -> p j b", j=JPAD),
                               ACT.Copy).then_inc(y_set, 1)

            def cin_features(k):
                act.wait_ge(l2_done, k + 1)
                act.activation(feat[:, 1, bass.ds(BLOCK_ROWS * k, BLOCK_ROWS)], y_sb[:, F, :],
                               ACT.Copy).then_inc(l1_feat_set, 1)
                act.activation(feat[:, 2, bass.ds(BLOCK_ROWS * k, BLOCK_ROWS)], ps_y[:, 0:BLOCK_ROWS],
                               ACT.Identity, bias=b2_d[:, 0:1]).then_inc(l2_feat_set, 1)

            def block_of(k, first, prepares):
                for p in range(SLOTS):
                    s, q = divmod(p, BANKS)
                    g = TILES * k + s
                    if q in ACT_BANKS:
                        n = ACT_BANKS.index(q)
                        if n == 0 and (s >= 2 or not first):
                            act.wait_ge(gp_steps, GP_STEPS * (g - 1))
                        if n == DVE_ADDS and (s >= 2 or not first):
                            act.wait_ge(joined, JOINS * (g - 2) + 2)
                        act.wait_ge(bank_done, BANKS * g + q + 1)
                        for x in range(JB):
                            j = JB * q + x
                            ins = act.activation(prod[:, s % 2, n, H * x:H * (x + 1)],
                                                 ps_t[(BANKS * s + q) % T_RING][:, H * x:H * (x + 1)],
                                                 ACT.Copy, scale=x0_t[:, s, j:j + 1])
                        ins.then_inc(act_scaled, 1)
                    if p - 1 + SLOTS in Y_AT and not first:
                        store_y(k - 1, Y_AT.index(p - 1 + SLOTS))
                    if p == L2_FROM + L2_SLOTS and not first:
                        cin_features(k - 1)
                    if p - 1 in Y_AT:
                        if p - 1 == Y_AT[0] and not first:
                            act.wait_ge(l1_feat_set, k)
                        store_y(k, Y_AT.index(p - 1))
                    for ahead, c, u in layer0_at(p):
                        if ahead == 0 or prepares:
                            layer0(k + ahead, c, u)
                    if prepares and p - 2 in TURN_AT:
                        turned(k + 1, TURN_AT.index(p - 2))

            act.wait_ge(w0_in, 16 * 2)
            act.wait_ge(w0_folded, 1)
            act.activation(w0_hi[:, :, :].rearrange("p t h -> p (t h)"), w0_fwd_raw, ACT.Copy).then_inc(w0_split, 1)
            act.wait_ge(consts_in, 16 * 4)
            act.activation(b0_d[:, :], b0_sb[:, :], ACT.Copy, scale=float(D)).then_inc(bias_scaled, 1)
            act.activation(b2_d[:, :], b2_sb[:, :], ACT.Copy, scale=float(D)).then_inc(bias_scaled, 1)
            act.wait_ge(w1_in, 16)
            act.activation(w1_hi[:, :], w1_raw, ACT.Copy).then_inc(w1_hi_set, 1)
            act.wait_ge(bias_scaled, 2)
            for r in range(ETR):
                turned(0, r)
            for c, u in layer0_first():
                layer0(0, c, u)
            act.wait_ge(w1_split, 1)
            act.wait_ge(w0_split, 2)
            block_of(0, True, True)
            with act.Fori(1, BLOCKS - 1) as k:
                block_of(k, False, True)
            block_of(BLOCKS - 1, False, False)
            def hidden(n, source, target, bias):
                act.wait_ge(top_mm, n)
                act.activation(target, source, ACT.Relu, bias=bias).then_inc(top_act, 1)

            act.wait_ge(top_in, 16 * 6)
            act.wait_ge(joined, JOINS * (TILES * BLOCKS - 1))
            for m in range(TOP1 // P):
                hidden(m + 1, ps_t[m][:, :], h1[0][:, m, :], bt1[:, m:m + 1])
                if m == 1:
                    store_y(BLOCKS - 1, TILES - 2)
            store_y(BLOCKS - 1, TILES - 1)
            cin_features(BLOCKS - 1)
            for m in range(TOP1 // P):
                hidden(TOP1 // P + m + 1, ps_t[m][:, :], h1[1][:, m, :], bt1[:, m:m + 1])
            for half in range(2):
                for m in range(TOP2 // P):
                    n = 2 * TOP1 // P + half * TOP2 // P + m + 1
                    hidden(n, top2_banks[half][m][:, :], h2[half][:, m, :], bt2[:, m:m + 1])
            for half in range(2):
                act.wait_ge(top_mm, TOP_STEPS - 1 + half)
                act.activation(y_out[:, HALF * half:HALF * half + HALF], top3_banks[half][0:1, :],
                               ACT.Copy).then_inc(top_act, 1)

        @block.vector
        def _(dve):
            def layer0(k, c, u):
                chunk = CHUNKS * k + c
                cols = slice(c * CHUNK, (c + 1) * CHUNK)
                known = once(chunk)
                t, r = divmod(u - Z_AT, STEP)
                if r == 0 and 0 <= t < UNITS:
                    n = UNITS * chunk + t
                    b = (c * UNITS + t) % Z_RING
                    if t == 0:
                        dve.wait_ge(copies_in[c % 2], 16 * COPIES * (2 * k + c // 2 + 1))
                    if not (known and n < Z_RING):
                        was, tw = ring_before(chunk, t)
                        dve.wait_ge(z_lo_set(tw), low_part_count(was, tw))
                    place = (UNITS * c + t) % A_RING
                    fills = UNITS * CHUNKS // A_RING * k + (UNITS * c + t) // A_RING + 1
                    dve.wait_ge(shifted_in[place], 16 * COPIES * fills)
                    dve.tensor_tensor(z[:, b, :], x0_shifted[:, place, :], x0_copies[:, c % 2, :],
                                      ALU.mult).then_inc(z_set, 1)
                t, r = divmod(u - Z_LO_AT, STEP)
                if r == 0 and t in DVE_LOW:
                    n = UNITS * chunk + t
                    b = (c * UNITS + t) % Z_RING
                    dve.wait_ge(z_hi_set, n + 1)
                    if not (known and n < Z_RING):
                        dve.wait_ge(z_used, n - Z_RING + 1)
                    dve.tensor_tensor(z_lo[:, b, :], z[:, b, :], z_hi[:, b, :].bitcast(F32),
                                      ALU.subtract).then_inc(z_lo_dve, 1)
                if u == X1_LO_AT:
                    dve.wait_ge(x1_hi_set, chunk + 1)
                    dve.scalar_tensor_tensor(x1_lo[:, cols], ps_x1[:, :], b0_sb[:, 0:1], x1_hi[:, cols].bitcast(F32),
                                             ALU.add, ALU.subtract).then_inc(x1_done, 1)
                    dve.tensor_reduce(feat[:, 0, bass.ds(BLOCK_ROWS * k + CHUNK // D * c, CHUNK // D)],
                                      ps_x1[:, :].rearrange("p (b d) -> p b d", d=D), AX.X,
                                      ALU.add).then_inc(x1_done, 1)

            def join(k, s, step, early):
                g = TILES * k + s
                mine = dve_sum[:, s % 2].rearrange("p a h -> p (a h)")
                if step == 0:
                    dve.wait_ge(dve_steps, DVE_UNITS * (g + 1))
                    dve.wait_ge(act_scaled, len(ACT_BANKS) * g + DVE_ADDS + 1)
                else:
                    dve.wait_ge(joined, JOINS * g + step)
                if step < 2:
                    dve.tensor_tensor(mine, mine, prod[:, s % 2, DVE_ADDS, 2 * H * step:2 * H * (step + 1)],
                                      ALU.add).then_inc(joined, 1)
                elif step == 2:
                    dve.wait_ge(gp_steps, GP_STEPS * (g + 1))
                    dve.tensor_tensor(mine, mine, gp_sum[:, s % 2].rearrange("p a h -> p (a h)"),
                                      ALU.add).then_inc(joined, 1)
                else:
                    if not early:
                        dve.wait_ge(y_done, g - 3)
                    dve.tensor_tensor(x2[:, s % 4, :], dve_sum[:, s % 2, 0, :], dve_sum[:, s % 2, 1, :],
                                      ALU.add).then_inc(joined, 1)

            def block_of(k, first, prepares):
                for p in range(SLOTS):
                    s, q = divmod(p, BANKS)
                    g = TILES * k + s
                    if q in DVE_BANKS:
                        if q == DVE_BANKS[0] and s % TPC == 0:
                            dve.wait_ge(x0_t_set, CHUNKS * k + s // TPC + 1)
                        for x in range(FIELDS_OF[q]):
                            n = dve_units_before(q) + x
                            j = JB * q + x
                            mine = dve_sum[:, s % 2, n % 2, :]
                            t_j = ps_t[(BANKS * s + q) % T_RING][:, H * x:H * (x + 1)]
                            if n >= 2:
                                dve.wait_ge(dve_steps, DVE_UNITS * g + n - 1)
                            elif n == 0 and (s >= 2 or not first):
                                dve.wait_ge(joined, JOINS * (g - 1))
                            if x == 0:
                                dve.wait_ge(bank_done, BANKS * g + q + 1)
                            if n == 1:
                                dve.tensor_scalar(mine, t_j, x0_t[:, s, j:j + 1], None, ALU.mult).then_inc(dve_steps, 1)
                            else:
                                dve.scalar_tensor_tensor(mine, t_j, x0_t[:, s, j:j + 1], b1_sb[:, :] if n == 0 else mine,
                                                         ALU.mult, ALU.add).then_inc(dve_steps, 1)
                    if q in JOIN_AT and s > 0:
                        join(k, s - 1, JOIN_AT.index(q), first and s - 1 < 4)
                    if q in JOIN_AT and s == 0 and not first:
                        join(k - 1, TILES - 1, JOIN_AT.index(q), False)
                    for ahead, c, u in layer0_at(p):
                        if ahead == 0 or prepares:
                            layer0(k + ahead, c, u)

            def layer0_bias(half):
                mine = feat[:, 0, HALF * half:HALF * half + HALF]
                dve.wait_ge(x1_done, CHUNKS * BLOCKS * (half + 1))
                dve.wait_ge(bias_scaled, 2)
                dve.tensor_scalar(mine, mine, b0_d[:, 0:1], None, ALU.add).then_inc(feat0_done, 1)

            dve.wait_ge(w0_in, 16 * 2)
            dve.tensor_tensor(w0_fwd_raw, w0_fwd_raw, w0_rev_raw, ALU.add).then_inc(w0_folded, 1)
            dve.wait_ge(w0_split, 1)
            dve.tensor_tensor(w0_lo[:, :, :].rearrange("p t h -> p (t h)"), w0_fwd_raw,
                              w0_hi[:, :, :].rearrange("p t h -> p (t h)").bitcast(F32),
                              ALU.subtract).then_inc(w0_split, 1)
            dve.wait_ge(w1_hi_set, 1)
            dve.tensor_tensor(w1_lo[:, :], w1_raw, w1_hi[:, :].bitcast(F32), ALU.subtract).then_inc(w1_split, 1)
            dve.wait_ge(consts_in, 16 * 4)
            for c, u in layer0_first():
                layer0(0, c, u)
            block_of(0, True, True)
            with dve.Fori(1, BLOCKS - 1) as k:
                block_of(k, False, True)
            layer0_bias(0)
            block_of(BLOCKS - 1, False, False)
            for step in range(JOINS):
                join(BLOCKS - 1, TILES - 1, step, False)
            layer0_bias(1)

        @block.tensor
        def _(pe):
            def turn(k, r):
                if r == 0:
                    if not (once(k) and k == 0):
                        pe.wait_ge(x0_t_set, CHUNKS * k)
                    pe.wait_ge(emb_in, 16 * F * (k + 1))
                elif not (once(k) and k == 0):
                    pe.wait_ge(x0_set, ETR * k + r)
                pe.nop(nofuse=True)
                for x in range(4):
                    ins = pe.transpose(turn_bank(k, r)[0:F, BLOCK_ROWS * x:BLOCK_ROWS * (x + 1)],
                                       emb[:, :].rearrange("p (j d) -> p d j", d=D)[:, 4 * r + x, :],
                                       ident_sb[:, :])
                ins.then_inc(emb_turned, 1)

            def layer0(k, c, u):
                chunk = CHUNKS * k + c
                known = once(chunk)
                if u == X0_TURN_AT:
                    if c == 0:
                        pe.wait_ge(x0_set, ETR * (k + 1))
                    else:
                        pe.wait_ge(x0_t_set, chunk)
                    pe.wait_ge(copies_in[c % 2], 16 * COPIES * (2 * k + c // 2 + 1))
                    for t in range(TPC):
                        ins = pe.transpose(ps_turn[:, P * t:P * t + PAIRS], x0_copies[:, c % 2, P * t:P * (t + 1)],
                                           ident_sb[0:PAIRS, 0:PAIRS])
                    ins.then_inc(x0_turned, 1)
                t, r = divmod(u - SUM_AT, STEP)
                if r == 0 and 0 <= t < UNITS:
                    n = UNITS * chunk + t
                    b = (c * UNITS + t) % Z_RING
                    if t == 0 and not (known and chunk == 0):
                        pe.wait_ge(x1_done, 2 * chunk)
                    pe.wait_ge(z_lo_set(t), low_part_count(chunk, t))
                    pe.matmul(ps_x1[:, :], w0_hi[:, t, :], z_hi[:, b, :], start=(t == 0), stop=False)
                    pe.matmul(ps_x1[:, :], w0_lo[:, t, :], z_hi[:, b, :], start=False, stop=False)
                    pe.matmul(ps_x1[:, :], w0_hi[:, t, :], z_lo[:, b, :], start=False,
                              stop=(t == UNITS - 1)).then_inc(z_used, 1)

            def sum_over_d(k, s):
                g = TILES * k + s
                c = s // TPC
                if s % TPC == 0:
                    pe.wait_ge(diag_in[c % 2], 16 * TILE_ROWS * (2 * k + c // 2 + 1))
                if s > 0:
                    pe.wait_ge(y_set, g)
                elif not (once(k) and k == 0):
                    pe.wait_ge(l2_feat_set, k)
                pe.wait_ge(joined, JOINS * (g + 1))
                pe.matmul(ps_y[:, 0:TILE_ROWS * JPAD], x2[:, s % 4, :],
                          x0_diag[:, s % DIAG_RING].rearrange("p b j -> p (b j)"), start=True, stop=True).then_inc(y_done, 1)

            def layer2(k, j):
                if j == 0:
                    pe.wait_ge(y_set, TILES * (k + 1))
                ins = pe.matmul(ps_y[:, 0:BLOCK_ROWS], w2_sb[:, j, :], y_sb[:, j, :], start=(j == 0), stop=(j == F - 1))
                if j == F - 1:
                    ins.then_inc(l2_done, 1)

            def bank_free(k, p):
                so, qo = divmod(p - T_RING, BANKS)
                go = TILES * k + so
                if qo in ACT_BANKS:
                    pe.wait_ge(act_scaled, len(ACT_BANKS) * go + ACT_BANKS.index(qo) + 1)
                else:
                    pe.wait_ge(dve_steps, DVE_UNITS * go + dve_units_before(qo + 1))

            def block_of(k, first, prepares):
                for p in range(SLOTS):
                    s, q = divmod(p, BANKS)
                    if q == 0 and s % TPC == 0:
                        pe.wait_ge(x1_done, 2 * (CHUNKS * k + s // TPC) + 1)
                    if not (first and p < T_RING):
                        bank_free(k, p)
                    w = FIELDS_OF[q] * H
                    ps = ps_t[p % T_RING][:, 0:w]
                    cols = slice(P * s, P * (s + 1))
                    js = slice(JB * H * q, JB * H * q + w)
                    pe.matmul(ps, x1_hi[:, cols], w1_hi[:, js], start=True, stop=False)
                    pe.matmul(ps, x1_hi[:, cols], w1_lo[:, js], start=False, stop=False)
                    pe.matmul(ps, x1_lo[:, cols], w1_hi[:, js], start=False, stop=True).then_inc(bank_done, 1)
                    if p + SLOTS in Y_AT and not first:
                        sum_over_d(k - 1, Y_AT.index(p + SLOTS))
                    if p in Y_AT:
                        sum_over_d(k, Y_AT.index(p))
                    if not first and L2_FROM <= p < L2_FROM + L2_SLOTS:
                        for j in range(L2_EACH * (p - L2_FROM), min(F, L2_EACH * (p - L2_FROM + 1))):
                            layer2(k - 1, j)
                    for ahead, c, u in layer0_at(p):
                        if ahead == 0 or prepares:
                            layer0(k + ahead, c, u)
                    if prepares and p in TURN_AT:
                        turn(k + 1, TURN_AT.index(p))

            pe.wait_ge(consts_in, 16 * 4)
            for r in range(ETR):
                turn(0, r)
            pe.wait_ge(w0_split, 2)
            for c, u in layer0_first():
                layer0(0, c, u)
            pe.wait_ge(w1_split, 1)
            block_of(0, True, True)
            pe.wait_ge(w2_in, 16)
            with pe.Fori(1, BLOCKS - 1) as k:
                block_of(k, False, True)
            block_of(BLOCKS - 1, False, False)

            def top1(half, m):
                rows = slice(HALF * half, HALF * half + HALF)
                for n in range(N_CIN):
                    pe.matmul(ps_t[m][:, :], wt1[:, n, P * m:P * (m + 1)], feat[:, n, rows], start=(n == 0), stop=False)
                pe.matmul(ps_t[m][:, :], wt1_dense[:, P * m:P * (m + 1)], dense[:, rows], start=False,
                          stop=True).then_inc(top_mm, 1)

            pe.wait_ge(top_in, 16 * 6)
            pe.wait_ge(feat0_done, 1)
            pe.wait_ge(l2_feat_set, BLOCKS // 2)
            for m in range(TOP1 // P):
                bank_free(BLOCKS - 1, SLOTS + m)
                top1(0, m)
                if m == 1:
                    sum_over_d(BLOCKS - 1, TILES - 2)
            sum_over_d(BLOCKS - 1, TILES - 1)
            for j in range(F):
                layer2(BLOCKS - 1, j)
            pe.wait_ge(feat0_done, 2)
            pe.wait_ge(l2_feat_set, BLOCKS)
            for m in range(TOP1 // P):
                pe.wait_ge(top_act, m + 1)
                top1(1, m)
            pe.wait_ge(wt2_in, 16)
            for half in range(2):
                for m in range(TOP2 // P):
                    if half == 0:
                        pe.wait_ge(top_act, TOP1 // P)
                    elif m == 0:
                        bank_free(BLOCKS - 1, SLOTS + 4)
                    else:
                        pe.wait_ge(top_act, TOP1 // P + 1)
                    if half == 1:
                        pe.wait_ge(top_act, 2 * TOP1 // P)
                    for n in range(TOP1 // P):
                        ins = pe.matmul(top2_banks[half][m][:, :], wt2[:, n, P * m:P * (m + 1)], h1[half][:, n, :],
                                        start=(n == 0), stop=(n == TOP1 // P - 1))
                    ins.then_inc(top_mm, 1)
            for half in range(2):
                pe.wait_ge(top_act, 2 * TOP1 // P + (half + 1) * TOP2 // P)
                for n in range(TOP2 // P):
                    ins = pe.matmul(top3_banks[half][0:1, :], wt3[:, n:n + 1], h2[half][:, n, :],
                                    start=(n == 0), stop=(n == TOP2 // P - 1))
                ins.then_inc(top_mm, 1)


def _pair_layout(w, reverse):
    import numpy as np
    o = np.zeros((COPIES, F, UNITS, H), w.dtype)
    j = np.arange(F)
    for t in range(UNITS):
        for g in range(COPIES):
            s = COPIES * t + g
            if s > F // 2 or (reverse and s == 0):
                continue
            k = (j + s) % F
            o[g, :, t, :] = (w[:, k, j] if reverse else w[:, j, k]).T
    return o.reshape(PAIRS, UNITS * H)


def kernel(**inputs):
    import numpy as np
    import concourse.bacc as _bacc
    from concourse import mybir as _mybir
    from concourse.bass_utils import run_bass_kernel_spmd as _run

    a = {n: np.asarray(v) for n, v in inputs.items()}
    mask = np.zeros((P, TILE_ROWS, JPAD), np.float32)
    for p in range(P):
        mask[p, p // D, F] = 1.0
    arrays = {
        "ids": a["ids"].reshape(BLOCKS, BLOCK_ROWS, F),
        "dense_t": a["dense_ctx"].T,
        "w0_fwd": _pair_layout(a["L0_rec_W0"].reshape(H, F, F), False),
        "w0_rev": _pair_layout(a["L0_rec_W0"].reshape(H, F, F), True),
        "w1": a["L0_rec_W1"].reshape(H, F, H).transpose(2, 1, 0).reshape(H, F * H),
        "w2": a["L0_rec_W2"].reshape(H, F, H).transpose(2, 1, 0),
        "b0": a["L0_rec_b0"].reshape(H, 1),
        "b1_rows": np.broadcast_to(a["L0_rec_b1"], (P, H)),
        "b2": a["L0_rec_b2"].reshape(H, 1),
        "ident": np.eye(P, dtype=np.float32),
        "mask": mask,
        "w_top1": a["W_top1"][:N_CIN * H].reshape(N_CIN, H, TOP1).transpose(1, 0, 2),
        "w_top1_dense": a["W_top1"][N_CIN * H:],
        "b_top1": a["b_top1"].reshape(TOP1 // P, P).T,
        "w_top2": a["W_top2"].reshape(TOP1 // P, P, TOP2).transpose(1, 0, 2),
        "b_top2": a["b_top2"].reshape(TOP2 // P, P).T,
        "w_top3": a["W_top3"].reshape(TOP2 // P, P).T,
    }
    for f in range(F):
        arrays[f"tbl_{f}"] = a[f"tbl_{f}"]
    nc = _bacc.Bacc("TRN2", target_bir_lowering=False, num_devices=1)
    args, maps = {}, {}
    for n, v in arrays.items():
        v = np.ascontiguousarray(v)
        maps[f"in_{n}"] = v
        args[n] = nc.dram_tensor(f"in_{n}", v.shape, _mybir.dt.from_np(v.dtype), kind="ExternalInput").ap()
    tables = [args.pop(f"tbl_{f}") for f in range(F)]
    out = nc.dram_tensor("out_0", (B, 1), _mybir.dt.float32, kind="ExternalOutput").ap()
    cin_tower(nc, **args, out=out, tables=tables)
    return _run(nc, [maps], core_ids=[0]).results[0]["out_0"]
```
